# Optimizing a Trainium2 kernel written in Bass

```python
import numpy as np
import jax
import jax.numpy as jnp

def _softmax(x, axis=-1):
    return jax.nn.softmax(x, axis=axis)

def _gelu(x):
    return jax.nn.gelu(x, approximate=True)

def _silu(x):
    return jax.nn.silu(x)

def _sigmoid(x):
    return jax.nn.sigmoid(x)

def _layernorm(x, axis=-1, eps=1e-05):
    m = jnp.mean(x, axis=axis, keepdims=True)
    v = jnp.var(x, axis=axis, keepdims=True)
    return (x - m) / jnp.sqrt(v + eps)

def _scatter_add(tgt, idx, src, axis=0):
    return tgt.at[idx].add(src)

def _segment_sum(src, seg, n):
    return jax.ops.segment_sum(src, seg, n)
kernel_name = 'mk_flamingo_gated_d1_seqx_r2_2d80bf'

def setup_inputs(seed: int=0):
    np.random.seed(seed)
    _w = jnp.asarray

    def _rec_inputs():
        import jax
        import jax.numpy as jnp
        _rk = jax.random.key(seed)
        x = -0.0003929 + 0.9999 * jax.random.normal(jax.random.fold_in(_rk, 1), (16, 224, 2048), jnp.float32)
        _lenS = 224 - jax.random.randint(jax.random.fold_in(_rk, 7), (16,), 0, max(1, 224 // 4) + 1, jnp.int32)
        _lenS2 = 750 - jax.random.randint(jax.random.fold_in(_rk, 8), (16,), 0, max(1, 750 // 4) + 1, jnp.int32)
        _ctx_1024P = jax.random.normal(jax.random.fold_in(_rk, 11), (16, 16, 512), jnp.float32)
        _ctx_1024c = jax.random.dirichlet(jax.random.fold_in(_rk, 511), 0.3 * jnp.ones((16,), jnp.float32), (16, 750))
        _ctx_1024t = jnp.einsum('bsk,bkd->bsd', _ctx_1024c, _ctx_1024P)
        _ctx_1024t = _ctx_1024t * jax.lax.rsqrt(jnp.mean(jnp.square(_ctx_1024t)) + 1e-12) * 0.953939
        ctx_1024 = -1.39393e-06 + 0.999914 * (_ctx_1024t + 0.3 * jax.random.normal(jax.random.fold_in(_rk, 611), (16, 750, 512), jnp.float32))
        _validS = jnp.arange(224)[None, :] < _lenS[:, None]
        _validS2 = jnp.arange(750)[None, :] < _lenS2[:, None]
        _causal = jnp.tril(jnp.ones((224, 224), dtype=bool))
        mask_SxS2_ff0 = jnp.where(jnp.ones((224, 750), dtype=bool), 0.0, -1000000000.0).astype(jnp.float32)
        _g = jax.random.normal(jax.random.fold_in(_rk, 9001), (2, 1), jnp.float32)
        _g = jnp.sign(_g) * jnp.maximum(jnp.abs(_g), 1.0) + (_g == 0) * 1.0
        g_xattn = _g[0]
        g_ffn = _g[1]
        return (x, ctx_1024, mask_SxS2_ff0, g_xattn, g_ffn)
    x, ctx_1024, mask_SxS2_ff0, g_xattn, g_ffn = _rec_inputs()

    def _L0_xattn_setup():
        import math
        import jax, jax.numpy as jnp
        import numpy as np
        N_HEADS = 32
        N_KV_HEADS = 8
        N_REP = N_HEADS // N_KV_HEADS
        HEAD_DIM = 2048 // N_HEADS
        key = jax.random.key(seed)
        kq, kk, kv = jax.random.split(key, 3)
        B, S, T = (2, 1024, 1024)
        q = jax.random.normal(kq, (B, S, N_HEADS * HEAD_DIM), dtype=jnp.float32)
        k = jax.random.normal(kk, (B, T, N_KV_HEADS * HEAD_DIM), dtype=jnp.float32)
        v = jax.random.normal(kv, (B, T, N_KV_HEADS * HEAD_DIM), dtype=jnp.float32)
        mask = jnp.zeros((S, T), dtype=jnp.float32)
        return {'q': q, 'k': k, 'v': v, 'start_pos': 0, 'mask': mask}
    _L0_xattn_all = _L0_xattn_setup()
    _L0_xattn_in = {k: v for k, v in _L0_xattn_all.items() if k in ()}
    del _L0_xattn_all

    def _L0_ffn_setup():
        import jax, jax.numpy as jnp
        import numpy as np
        B, L, H, Dh, M = (4, 1024, 16, 128, 512)
        D = H * Dh
        key = jax.random.key(seed)
        kx, ku, kd, kp = jax.random.split(key, 4)
        x = jax.random.normal(kx, (B, L, D), dtype=jnp.float32)
        up = jax.random.normal(ku, (H, Dh, M), dtype=jnp.float32)
        down = jax.random.normal(kd, (H, M, Dh), dtype=jnp.float32)
        perm = jax.random.permutation(kp, D)
        return {'x': x, 'up': up, 'down': down, 'perm': perm}
    _L0_ffn_all = _L0_ffn_setup()
    _L0_ffn_in = {k: v for k, v in _L0_ffn_all.items() if k in ('up', 'down', 'perm')}
    del _L0_ffn_all
    return {'x': x, 'ctx_1024': ctx_1024, 'mask_SxS2_ff0': mask_SxS2_ff0, 'g_xattn': g_xattn, 'g_ffn': g_ffn, 'L0_ffn_up': _L0_ffn_in['up'], 'L0_ffn_down': _L0_ffn_in['down'], 'L0_ffn_perm': _L0_ffn_in['perm']}

def reference(x, ctx_1024, mask_SxS2_ff0, g_xattn, g_ffn, L0_ffn_up, L0_ffn_down, L0_ffn_perm):
    import jax
    import jax.numpy as jnp

    def _L0_xattn_ref(q, k, v, start_pos, mask):
        import math
        import jax, jax.numpy as jnp
        import numpy as np
        N_HEADS = 32
        N_KV_HEADS = 8
        N_REP = N_HEADS // N_KV_HEADS
        HEAD_DIM = 2048 // N_HEADS
        b, s, _ = q.shape
        t = k.shape[1]
        xq = q.reshape(b, s, N_KV_HEADS, N_REP, HEAD_DIM)
        xk = k.reshape(b, t, N_KV_HEADS, HEAD_DIM)
        xv = v.reshape(b, t, N_KV_HEADS, HEAD_DIM)
        scores = jnp.einsum('bsgrd,btgd->bgrst', xq, xk) / math.sqrt(HEAD_DIM)
        scores = scores + mask
        probs = jax.nn.softmax(scores.astype(jnp.float32), axis=-1).astype(q.dtype)
        out = jnp.einsum('bgrst,btgd->bsgrd', probs, xv)
        return out.reshape(b, s, N_HEADS * HEAD_DIM)

    def _L0_ffn_ref(x, up, down, perm):
        import jax, jax.numpy as jnp
        import numpy as np
        B, L, H, Dh, M = (4, 1024, 16, 128, 512)
        D = H * Dh
        b, l, Dm = x.shape
        h, d = (up.shape[0], up.shape[1])
        unperm = jnp.argsort(perm)
        t = x.reshape(b * l, Dm)
        t = t[:, perm]
        t = t.reshape(b * l, h, d)
        t = jnp.einsum('bhd,hdm->bhm', t, up)
        t = jax.nn.gelu(t, approximate=False)
        t = jnp.einsum('bhm,hmd->bhd', t, down)
        t = t.reshape(b * l, h * d)
        t = t[:, unperm]
        out = t.reshape(b, l, Dm)
        return out
    x = x + jnp.tanh(g_xattn[0]) * _L0_xattn_ref(_layernorm(x, axis=-1), ctx_1024, ctx_1024, 0, mask_SxS2_ff0)
    x = x + jnp.tanh(g_ffn[0]) * _L0_ffn_ref(_layernorm(x, axis=-1), L0_ffn_up, L0_ffn_down, L0_ffn_perm)
    return x

_drawn_inputs = setup_inputs


def setup_inputs(seed=0):
    import zlib

    import numpy as np

    out = dict(_drawn_inputs(seed))
    spreads = {'mask_SxS2_ff0': (0.0, 0.8)}
    factors = {}
    for name, (base, spread) in spreads.items():
        noise = np.random.default_rng([zlib.crc32(name.encode()), seed]).standard_normal(out[name].shape)
        drawn = base * np.exp(spread * noise) if base else spread * noise
        out[name] = jnp.asarray(drawn.astype(out[name].dtype))
    for name, factor in factors.items():
        out[name] = (out[name] * factor).astype(out[name].dtype)
    return out
```

```python
from contextlib import ExitStack

import concourse.bass as bass
from concourse import mybir

F32 = mybir.dt.float32
F32R = mybir.dt.float32r
I32 = mybir.dt.int32
U32 = mybir.dt.uint32
ALU = mybir.AluOpType
ACT = mybir.ActivationFunctionType
AX_X = mybir.AxisListType.X

P = 128
B, SQ, D = 16, 224, 2048
T, C = 750, 512
NG, NR, DH = 8, 4, 64
ROWS = B * SQ
PJ = P // NR
NJ = SQ // PJ
NT, TT = 6, T // 6
NPAIR = NG // 2
PAIRS = B * NPAIR
CH = (4, 3)
QW = NJ * P
EPS = 1e-5
STEPS = 7
HALF = NT // 2
H, M = 16, 512
MC = M // P
COLS, NC = 448, 8
INV = 1.0 / 8.0


def build(nc, x, ctx_in, mask, g_x, g_f, up, down, perm, out):
    x1t_dram = nc.dram_tensor("x1t_scratch", [D, ROWS], F32).ap()
    zt_dram = nc.dram_tensor("zt_scratch", [D, ROWS], F32).ap()
    stat_dram = nc.dram_tensor("stat_scratch", [2, ROWS], F32).ap()

    with ExitStack() as keep:
        consts = {
            "ident": keep.enter_context(nc.sbuf_tensor("ident", [P, P], F32)),
            "gate": keep.enter_context(nc.sbuf_tensor("gate", [P, 2], F32)),
        }
        attention(nc, x, ctx_in, mask, g_x, g_f, consts, x1t_dram, stat_dram)
        feed_forward(nc, up, down, perm, consts, x1t_dram, stat_dram, zt_dram)
        transpose_back(nc, consts, zt_dram, out)


def attention(nc, x, ctx_in, mask, g_x, g_f, consts, x1t_dram, stat_dram):
    ident, gate = consts["ident"], consts["gate"]
    x_view = x.rearrange("b (p j) (g r d) -> b r p j g d", j=NJ, g=NG, r=NR)
    ctx_view = ctx_in.rearrange("b (t p) c -> b p t c", p=TT)
    mask_view = mask.rearrange("(p j) t -> p j t", j=NJ)
    x1t_view = x1t_dram.rearrange("(n gg r d) c -> n gg d r c", n=NPAIR, gg=2, r=NR)
    stat_view = stat_dram.rearrange("s (b p j) -> s p b j", b=B, j=NJ)

    with ExitStack() as es:
        def sb(name, shape, dt=F32):
            return es.enter_context(nc.sbuf_tensor(name, shape, dt))

        def ps(name, cols):
            return es.enter_context(nc.psum_tensor(name, [P, cols], F32))

        def sem(name):
            return es.enter_context(nc.semaphore(name))

        mask_sb = sb("mask_sb", [P, NJ, T])
        x_raw = sb("x_raw", [P, 2, NJ, NG, DH])
        ctx_sb = sb("ctx_sb", [TT, 2, NT, C])
        k_split = sb("k_split", [TT, NT, 4, DH], F32R)
        values = [sb(f"values{i}", [TT, NT, 2 * DH], F32R) for i in range(2)]
        q_split = [sb(f"q_split{i}", [P, NJ, 2 * DH], F32R) for i in range(2)]
        qt = [sb(f"qt{i}", [P, QW], F32R) for i in range(2)]
        kt = [sb(f"kt{i}", [P, 2, T], F32R) for i in range(2)]
        neg_scores = [sb(f"neg_scores{i}", [P, T]) for i in range(2)]
        probs = [sb(f"probs{i}", [P, T]) for i in range(2)]
        pt_hi = [sb(f"pt_hi{c}", [TT, CH[c], NT, P], F32R) for c in range(2)]
        pt_lo = [sb(f"pt_lo{c}", [TT, CH[c], NT, P], F32R) for c in range(2)]
        att_t = sb("att_t", [P, QW])
        att_n = [sb(f"att_n{i}", [P, NJ, DH]) for i in range(2)]
        x1_pair = sb("x1_pair", [P, NJ, 2, DH])
        x1t_sb = sb("x1t_sb", [P, NR, PJ, NJ])
        xc = sb("xc", [P, NJ, DH])
        xn = sb("xn", [P, NJ, DH])
        neg_max = sb("neg_max", [P, 2 * NJ])
        row_sum = sb("row_sum", [P, 2, NJ])
        row_inv = sb("row_inv", [P, NJ])
        stats = sb("stats", [P, B, NJ, NPAIR, 6])
        mean = sb("mean", [P, B * NJ])
        rstd = sb("rstd", [P, B * NJ])
        var = sb("var", [P, B * NJ])
        part = sb("part", [P, B * NJ])
        power = sb("power", [P, B * NJ])
        same = sb("same", [P, P])
        fold = sb("fold", [P, DH])

        s_ps = [ps(f"s_ps{i}", 1024) for i in range(2)]
        pt_ps = [ps(f"pt_ps{i}", 512) for i in range(2)]
        o_ps = ps("o_ps", 512)
        m_ps = ps("m_ps", 512)

        gates_in = sem("gates_in")
        mask_in = sem("mask_in")
        stat_in = [sem(f"stat_in{i}") for i in range(2)]
        stat_taken = sem("stat_taken")
        zeroed = sem("zeroed")
        marked = sem("marked")
        gated = sem("gated")
        folded = sem("folded")
        powered = sem("powered")
        stat_v = sem("stat_v")
        stat_pe = sem("stat_pe")
        stat_done = sem("stat_done")
        x_arrived = sem("x_arrived")
        ctx_arrived = sem("ctx_arrived")
        k_cut = sem("k_cut")
        q_cut = sem("q_cut")
        v_put = sem("v_put")
        prep_filled = sem("prep_filled")
        prep_act = sem("prep_act")
        prep_dve = sem("prep_dve")
        scored = sem("scored")
        masked = sem("masked")
        expd = sem("expd")
        turned = [sem(f"turned{i}") for i in range(2)]
        hi_out = [sem(f"hi_out{i}") for i in range(2)]
        lo_out = [sem(f"lo_out{i}") for i in range(2)]
        weighed = sem("weighed")
        att_out = sem("att_out")
        summed = sem("summed")
        inverted = sem("inverted")
        normed = sem("normed")
        added = sem("added")
        x1_stat = sem("x1_stat")
        xt_filled = sem("xt_filled")
        xt_act = sem("xt_act")
        xt_dve = sem("xt_dve")
        x1_stored = sem("x1_stored")
        stat_stored = sem("stat_stored")
        dve_passed = sem("dve_passed")
        pool_passed = sem("pool_passed")
        sp_passed = sem("sp_passed")

        block = es.enter_context(nc.Block())

        def load_x(sp, b, par, s):
            for r in range(NR):
                sp.dma_start(x_raw[PJ * r:PJ * (r + 1), par], x_view[b, r]).then_inc(s, 16)

        def load_ctx(sp, b, par):
            sp.dma_start(ctx_sb[:, par], ctx_view[b]).then_inc(ctx_arrived, 16)

        @block.sync
        def _(sp):
            sp.dma_start(gate[:, 0:1], g_x.partition_broadcast(P)).then_inc(gates_in, 16)
            sp.dma_start(gate[:, 1:2], g_f.partition_broadcast(P)).then_inc(gates_in, 16)
            load_x(sp, 2, 0, stat_in[0])
            load_x(sp, 3, 1, stat_in[1])
            with sp.Fori(2, B // 2) as i:
                for par in range(2):
                    sp.wait_ge(stat_taken, (i - 2) * 2 + par + 1)
                    load_x(sp, i * 2 + par, par, stat_in[par])
            load_ctx(sp, 0, 0)
            sp.wait_ge(stat_taken, B - 3)
            load_x(sp, 0, 0, x_arrived)
            sp.wait_ge(ctx_arrived, 16)
            load_ctx(sp, 1, 1)
            sp.wait_ge(stat_taken, B - 2)
            sp.wait_ge(x_arrived, 64)
            load_x(sp, 1, 1, x_arrived)
            for r in range(NR):
                sp.dma_start(mask_sb[PJ * r:PJ * (r + 1)], mask_view).then_inc(mask_in, 16)

            def store_pair(b, n):
                u = b * NPAIR + n
                sp.wait_ge(xt_act, u + 1)
                sp.wait_ge(xt_dve, u + 1)
                for gg in range(2):
                    sp.dma_start(x1t_view[n, gg][:, :, bass.ds(b * SQ, SQ)],
                                 x1t_sb[DH * gg:DH * (gg + 1)].rearrange("p r q j -> p r (q j)")
                                 ).then_inc(x1_stored, 16)

            def store_batch(b):
                with sp.Fori(0, NPAIR) as n:
                    store_pair(b, n)

            with sp.Fori(0, B // 2 - 1) as i:
                for par in range(2):
                    b = i * 2 + par
                    store_batch(b)
                    sp.wait_ge(ctx_arrived, (b + 2) * 16)
                    sp.sem_inc(sp_passed, 1)
                    sp.wait_ge(k_cut, (b + 1) * (2 * NG))
                    load_ctx(sp, b + 2, par)
                    sp.wait_ge(x_arrived, (b + 2) * 64)
                    sp.sem_inc(sp_passed, 1)
                    sp.wait_ge(added, (b + 1) * NG)
                    load_x(sp, b + 2, par, x_arrived)
            for par in range(2):
                store_batch(B - 2 + par)
            sp.wait_ge(x1_stored, 32 * PAIRS)
            sp.wait_ge(stat_v, 2 * STEPS)
            sp.wait_ge(stat_done, 4)
            for k, t in enumerate((mean, rstd)):
                sp.dma_start(stat_view[k], t[0:PJ, :].rearrange("p (b j) -> p b j", j=NJ)).then_inc(stat_stored, 16)
            sp.wait_ge(stat_stored, 32)

        def ctx_group(g_no):
            return ctx_sb[:, (g_no >> 3) & 1, :, bass.ds((g_no & 7) * DH, DH)]

        def x_group(g_no):
            return x_raw[:, (g_no >> 3) & 1, :, g_no & 7, :]

        def of_batch(t, g_no):
            return t[:, bass.ds(((g_no >> 3) & (B - 1)) * NJ, NJ)].unsqueeze(2).to_broadcast([P, NJ, DH])


        @block.gpsimd
        def _(pool):
            pool.memset(ident[:, :], 0.0).then_inc(zeroed, 1)
            pool.memset(same[:, :], 0.0).then_inc(zeroed, 1)
            pool.memset(power[:, :], -0.5).then_inc(powered, 1)
            pool.wait_ge(zeroed, 2)
            pool.affine_select(out=ident[:, :], in_=ident[:, :], compare_op=ALU.not_equal, fill=1.0,
                               base=0, pattern=[[-1, P]], channel_multiplier=1).then_inc(marked, 1)
            for k in range(2 * NR - 1):
                pool.wait_ge(marked, k + 1)
                pool.affine_select(out=same[:, :], in_=same[:, :], compare_op=ALU.not_equal, fill=1.0,
                                   base=PJ * (k - NR + 1), pattern=[[-1, P]],
                                   channel_multiplier=1).then_inc(marked, 1)

            def reciprocal_deviation(k, scale):
                pool.wait_ge(stat_v, STEPS * (k + 1))
                pool.wait_ge(powered, 1)
                pool.tensor_tensor(rstd[:, :], var[:, :], power[:, :], ALU.pow).then_inc(stat_done, 1)
                pool.wait_ge(stat_done, 2 * k + 1)
                pool.tensor_scalar(rstd[:, :], rstd[:, :], scale, None, ALU.mult).then_inc(stat_done, 1)

            def cut_context(g_no, lag=True):
                pool.wait_ge(ctx_arrived, ((g_no >> 3) + 1) * 16)
                if lag:
                    pool.wait_ge(prep_filled, g_no * 5 - 1)
                    pool.wait_ge(v_put, g_no)
                src = ctx_group(g_no).unsqueeze(2).to_broadcast([TT, NT, 2, DH])
                pool.sem_inc(pool_passed, 1)
                pool.tensor_copy(k_split[:, :, 0:2, :], src).then_inc(k_cut, 1)
                pool.wait_ge(k_cut, g_no * 2 + 1)
                pool.sem_inc(pool_passed, 1)
                pool.tensor_tensor(k_split[:, :, 2:4, :], src, k_split[:, :, 0:2, :].bitcast(F32),
                                   ALU.subtract).then_inc(k_cut, 1)

            def cut_queries(g_no, slot, lag=True):
                pool.wait_ge(x_arrived, ((g_no >> 3) + 1) * 64)
                if lag:
                    pool.wait_ge(prep_filled, g_no * 5 - 5)
                    pool.wait_ge(q_cut, g_no * 4)
                dst = q_split[slot]
                pool.sem_inc(pool_passed, 1)
                pool.tensor_tensor(xc[:, :, :], x_group(g_no), of_batch(mean, g_no), ALU.subtract).then_inc(q_cut, 1)
                pool.wait_ge(q_cut, g_no * 4 + 1)
                pool.sem_inc(pool_passed, 1)
                pool.tensor_tensor(xn[:, :, :], xc[:, :, :], of_batch(rstd, g_no), ALU.mult).then_inc(q_cut, 1)
                pool.wait_ge(q_cut, g_no * 4 + 2)
                pool.sem_inc(pool_passed, 1)
                pool.tensor_copy(dst[:, :, 0:DH], xn[:, :, :]).then_inc(q_cut, 1)
                pool.wait_ge(q_cut, g_no * 4 + 3)
                pool.sem_inc(pool_passed, 1)
                pool.tensor_tensor(dst[:, :, DH:2 * DH], xn[:, :, :], dst[:, :, 0:DH].bitcast(F32),
                                   ALU.subtract).then_inc(q_cut, 1)

            def put_values(g_no, slot, lag=True):
                pool.wait_ge(k_cut, g_no * 2 + 2)
                if lag:
                    pool.wait_ge(weighed, g_no * 2 - 2)
                pool.sem_inc(pool_passed, 1)
                pool.tensor_copy(values[slot][:, :, :], k_split[:, :, 1:3, :].rearrange("p t s d -> p t (s d)").bitcast(F32)).then_inc(v_put, 1)

            def add_x(g_no, gg, lag=True):
                pool.wait_ge(normed, g_no + 1)
                if lag and gg == 0:
                    pool.wait_ge(xt_filled, g_no)
                    pool.wait_ge(x1_stat, g_no >> 1)
                pool.sem_inc(pool_passed, 1)
                pool.tensor_tensor(x1_pair[:, :, gg, :], att_n[gg][:, :, :], x_group(g_no),
                                   ALU.add).then_inc(added, 1)

            def pair(u, first=False, last=False):
                for gg in range(2):
                    g_no = u * 2 + gg
                    has_next = not (last and gg == 1)
                    if has_next:
                        cut_context(g_no + 1)
                    if not last:
                        cut_queries(g_no + 2, gg)
                    if has_next:
                        put_values(g_no + 1, 1 - gg, lag=not (first and gg == 0))
                    if not (first and gg == 0):
                        add_x(g_no - 1, 1 - gg, lag=not first)

            reciprocal_deviation(0, INV)
            pool.wait_ge(stat_done, 2)
            cut_context(0, lag=False)
            cut_queries(0, 0, lag=False)
            put_values(0, 0, lag=False)
            pool.wait_ge(q_cut, 4)
            cut_queries(1, 1, lag=False)
            pair(0, first=True)
            pair(1)
            with pool.Fori(2, PAIRS - 1) as u:
                pair(u)
            pair(PAIRS - 1, last=True)
            add_x(2 * PAIRS - 1, 1)
            reciprocal_deviation(1, 1.0)

        @block.tensor
        def _(pe):
            def sum_partitions(k):
                for step in range(2):
                    pe.wait_ge(stat_v, STEPS * k + (1, 6)[step])
                    if k == 0 and step == 0:
                        pe.wait_ge(marked, 2 * NR)
                    if k == 1 and step == 0:
                        pe.wait_ge(xt_dve, PAIRS)
                    pe.matmul(m_ps[:, 0:B * NJ], same[:, :], part[:, :], start=True, stop=True).then_inc(stat_pe, 1)

            def turn_queries(slot, piece):
                j0 = (0, CH[0])[piece]
                for j in range(CH[piece]):
                    last = pe.transpose(m_ps[:, j * P:(j + 1) * P], q_split[slot][:, j0 + j, :].bitcast(F32),
                                        ident[:, :])
                return last

            def turn_keys(k, col, t, part_no):
                src = k_split[:, t, 2 * part_no:2 * part_no + 2, :].rearrange("p s d -> p (s d)").bitcast(F32)
                return pe.transpose(m_ps[:, col * TT:(col + 1) * TT], src, ident[0:TT, 0:TT])

            def prep(g_no, slot, piece, first=False, after_sum=False):
                if piece == 0:
                    pe.wait_ge(q_cut, g_no * 4 + 4)
                    if not first:
                        pe.wait_ge(prep_act, g_no * 3)
                    last = turn_queries(slot, 0)
                elif piece == 1:
                    pe.wait_ge(k_cut, g_no * 2 + 2)
                    pe.wait_ge(prep_act, g_no * 3 + 1)
                    for t in range(4):
                        last = turn_keys(0, t, t, 0)
                elif piece == 2:
                    pe.wait_ge(prep_dve, g_no * 2 + 1)
                    for t in range(4):
                        last = turn_keys(0, t, t, 1)
                elif piece == 3:
                    pe.wait_ge(prep_act, g_no * 3 + 2)
                    for k in range(4):
                        last = turn_keys(0, k, 4 + k % 2, k // 2)
                else:
                    if after_sum:
                        pe.wait_ge(normed, g_no - 1)
                    else:
                        pe.wait_ge(prep_dve, g_no * 2 + 2)
                    last = turn_queries(slot, 1)
                last.then_inc(prep_filled, 1)

            def scores(g_no, slot, j, lag):
                n = g_no * NJ + j
                buf = (slot * NJ + j) % 2
                if j == 0:
                    pe.wait_ge(prep_act, g_no * 3 + 2)
                    pe.wait_ge(prep_dve, g_no * 2 + 2)
                if j == CH[0]:
                    pe.wait_ge(prep_act, g_no * 3 + 3)
                if lag or j >= 2:
                    pe.wait_ge(masked, n - 1)
                q = qt[slot][:, j * P:(j + 1) * P]
                for c0, c1 in ((0, 512), (512, T)):
                    pe.matmul(s_ps[buf][:, c0:c1], q, kt[slot][:, 0, c0:c1], start=True, stop=False)
                    last = pe.matmul(s_ps[buf][:, c0:c1], q, kt[slot][:, 1, c0:c1], start=False, stop=True)
                last.then_inc(scored, 1)

            def turn_probs(n, buf, lag):
                pe.wait_ge(expd, n + 1)
                for half in range(2):
                    if lag:
                        pe.wait_ge(lo_out[half], n)
                    for k in range(HALF):
                        t = half * HALF + k
                        last = pe.transpose(pt_ps[half][0:TT, k * P:(k + 1) * P],
                                            probs[buf][:, t * TT:(t + 1) * TT], ident[:, :])
                    last.then_inc(turned[half], 1)

            def weigh(g_no, slot, c, lag=True):
                width = CH[c] * P
                pe.wait_ge(lo_out[1], g_no * NJ + (CH[0], NJ)[c])
                pe.wait_ge(v_put, g_no + 1)
                if lag or c == 1:
                    pe.wait_ge(att_out, g_no * 2 + c)
                for t in range(NT):
                    for k, src in enumerate((pt_hi[c], pt_lo[c])):
                        last = pe.matmul(o_ps[:, 0:width], values[slot][:, t, :], src[:, :, t, :],
                                         start=(t == 0 and k == 0), stop=(t == NT - 1 and k == 1))
                last.then_inc(weighed, 1)

            def fold_parts(g_no):
                pe.wait_ge(att_out, g_no * 2 + 2)
                pe.wait_ge(folded, 2)
                for j in range(NJ):
                    last = pe.matmul(m_ps[:, j * DH:(j + 1) * DH], att_t[:, j * P:(j + 1) * P], fold[:, :],
                                     start=True, stop=True)
                last.then_inc(summed, 1)

            def turn_x1(u, piece):
                if piece == 0:
                    pe.wait_ge(added, u * 2 + 2)
                else:
                    pe.wait_ge(xt_act, u + 1)
                for j in range(CH[piece]):
                    last = pe.transpose(m_ps[:, j * P:(j + 1) * P],
                                        x1_pair[:, (0, CH[0])[piece] + j, :, :].rearrange("p g d -> p (g d)"),
                                        ident[:, :])
                last.then_inc(xt_filled, 1)

            def period(u, gg, new=True, lag=True, nxt=True, turn=True, first=False, second=False):
                g_no = u * 2 + gg
                for j in range(NJ):
                    n = g_no * NJ + j
                    if new:
                        scores(g_no, gg, j, lag)
                    if nxt and j < 4:
                        prep(g_no + 1, 1 - gg, j)
                    if gg == 1 and turn and j == 4:
                        if nxt:
                            pe.wait_ge(prep_dve, g_no * 2 + 4)
                        else:
                            pe.wait_ge(prep_act, g_no * 3 + 3)
                        turn_x1(u - 1, 0)
                    if gg == 1 and turn and j == 5:
                        turn_x1(u - 1, 1)
                    if nxt and j == 6:
                        prep(g_no + 1, 1 - gg, 4, after_sum=lag)
                    if (j >= 2 and new) or (j < 2 and lag):
                        turn_probs(n - 2, (gg * NJ + j) % 2, lag or j > 2)
                    if lag and j == 5:
                        if gg == 1 and turn:
                            pe.wait_ge(xt_dve, u)
                        elif nxt:
                            pe.wait_ge(prep_dve, g_no * 2 + 4)
                        else:
                            pe.wait_ge(normed, g_no - 1)
                        fold_parts(g_no - 1)
                    if lag and j in (0, 3):
                        weigh(g_no - 1, 1 - gg, j // 3, lag=not (first and gg == 1))

            sum_partitions(0)
            pe.wait_ge(stat_v, STEPS)
            for piece in range(5):
                prep(0, 0, piece, first=True)
            period(0, 0, lag=False, turn=False, first=True)
            period(0, 1, turn=False, first=True)
            period(1, 0, second=True)
            period(1, 1, second=True)
            with pe.Fori(2, PAIRS - 1) as u:
                period(u, 0)
                period(u, 1)
            period(PAIRS - 1, 0)
            period(PAIRS - 1, 1, nxt=False)
            period(PAIRS, 0, new=False, nxt=False, turn=False)
            pe.wait_ge(normed, 2 * PAIRS)
            for piece in range(2):
                turn_x1(PAIRS - 1, piece)
            sum_partitions(1)

        @block.scalar
        def _(act):
            act.wait_ge(gates_in, 32)
            act.activation(gate[:, :], gate[:, :], ACT.Tanh).then_inc(gated, 1)

            def prep_out(g_no, slot, piece, lag=True):
                act.wait_ge(prep_filled, g_no * 5 + piece + 1)
                if piece == 0:
                    last = act.activation(qt[slot][:, 0:CH[0] * P], m_ps[:, 0:CH[0] * P], ACT.Copy)
                elif piece == 2:
                    last = act.activation(kt[slot][:, 1, 0:4 * TT], m_ps[:, 0:4 * TT], ACT.Copy)
                else:
                    last = act.activation(qt[slot][:, CH[0] * P:QW], m_ps[:, 0:CH[1] * P], ACT.Copy)
                last.then_inc(prep_act, 1)

            def exponentials(n, s, lag):
                act.wait_ge(masked, n + 1)
                if lag:
                    act.wait_ge(turned[1], n - 1)
                act.activation(probs[s % 2][:, :], neg_scores[s % 2][:, :], ACT.Exp, bias=neg_max[:, s:s + 1],
                               scale=-1.0, accum_out=row_sum[:, s // NJ, s % NJ:s % NJ + 1]).then_inc(expd, 1)

            def hi_parts(g_no, j, lag):
                n = g_no * NJ + j
                c = int(j >= CH[0])
                if j in (0, CH[0]) and lag:
                    act.wait_ge(weighed, g_no * 2 - 1 + c)
                for half in range(2):
                    act.wait_ge(turned[half], n + 1)
                    act.activation(pt_hi[c][:, j - c * CH[0], half * HALF:(half + 1) * HALF, :],
                                   pt_ps[half][0:TT, 0:HALF * P], ACT.Copy).then_inc(hi_out[half], 1)

            def att_evacuate(g_no, c, lag=True):
                act.wait_ge(weighed, g_no * 2 + c + 1)
                if c == 0 and lag:
                    act.wait_ge(summed, g_no)
                act.activation(att_t[:, c * CH[0] * P:(c * CH[0] + CH[c]) * P], o_ps[:, 0:CH[c] * P],
                               ACT.Copy).then_inc(att_out, 1)

            def x1t_out(u, lag):
                act.wait_ge(xt_filled, u * 2 + 1)
                if lag:
                    act.wait_ge(x1_stored, u * 32)
                act.activation(x1t_sb[:, :, :, 0:CH[0]].rearrange("p r q j -> p j (r q)"),
                               m_ps[:, 0:CH[0] * P].rearrange("p (j c) -> p j c", c=P),
                               ACT.Copy).then_inc(xt_act, 1)

            def period(u, gg, new=True, lag=True, nxt=True, turn=True, first=False, second=False):
                g_no = u * 2 + gg
                for j in range(NJ):
                    n = g_no * NJ + j
                    if (j >= 1 and new) or (j < 1 and lag):
                        exponentials(n - 1, (gg * NJ + j - 1) % (2 * NJ), lag or j > 2)
                    if (j >= 2 and new) or (j < 2 and lag):
                        back = int(j < 2)
                        hi_parts(g_no - back, (j - 2) % NJ, not first or (gg == 1 and not back))
                    if nxt and j in (0, 2, 6):
                        prep_out(g_no + 1, 1 - gg, (0, 2, None, 4)[j // 2])
                    if lag and j in (1, 4):
                        att_evacuate(g_no - 1, j // 3, lag=not (first and gg == 1))
                    if gg == 1 and turn and j == 4:
                        x1t_out(u - 1, lag=not second)

            for piece in (0, 2, 4):
                prep_out(0, 0, piece)
            period(0, 0, lag=False, turn=False, first=True)
            period(0, 1, turn=False, first=True)
            period(1, 0, second=True)
            period(1, 1, second=True)
            with act.Fori(2, PAIRS - 1) as u:
                period(u, 0)
                period(u, 1)
            period(PAIRS - 1, 0)
            period(PAIRS - 1, 1, nxt=False)
            period(PAIRS, 0, new=False, nxt=False, turn=False)
            x1t_out(PAIRS - 1, True)

        @block.vector
        def _(dve):
            def combine(k, triples, count):
                n_parts = D // count
                base = STEPS * k
                mu = triples[:, :, :, 1]
                mean_wide = mean[:, :].unsqueeze(2).to_broadcast([P, B * NJ, n_parts // NR])
                dve.tensor_reduce(part[:, :], mu, AX_X, ALU.add).then_inc(stat_v, 1)
                dve.wait_ge(stat_pe, 2 * k + 1)
                dve.tensor_scalar(mean[:, :], m_ps[:, 0:B * NJ], 1.0 / n_parts, None, ALU.mult).then_inc(stat_v, 1)
                dve.wait_ge(stat_v, base + 2)
                dve.tensor_tensor(mu, mu, mean_wide, ALU.subtract).then_inc(stat_v, 1)
                dve.wait_ge(stat_v, base + 3)
                dve.tensor_tensor(mu, mu, mu, ALU.mult).then_inc(stat_v, 1)
                dve.wait_ge(stat_v, base + 4)
                dve.scalar_tensor_tensor(out=mu, in0=mu, scalar=float(count), in1=triples[:, :, :, 2],
                                         op0=ALU.mult, op1=ALU.add).then_inc(stat_v, 1)
                dve.wait_ge(stat_v, base + 5)
                dve.tensor_reduce(part[:, :], mu, AX_X, ALU.add).then_inc(stat_v, 1)
                dve.wait_ge(stat_pe, 2 * k + 2)
                dve.tensor_scalar(var[:, :], m_ps[:, 0:B * NJ], 1.0 / D, EPS, ALU.mult, ALU.add).then_inc(stat_v, 1)

            def take_stats(b, par, first=False):
                for j in range(NJ):
                    ins = dve.bn_stats(stats[:, b, j, 0, :], x_raw[:, par, j, :, :].rearrange("p g d -> p (g d)"))
                ins.then_inc(stat_taken, 1)

            dve.wait_ge(marked, 2 * NR)
            dve.tensor_tensor(fold[:, :], ident[:, 0:DH], ident[:, DH:P], ALU.add).then_inc(folded, 1)
            dve.wait_ge(gated, 1)
            dve.wait_ge(folded, 1)
            dve.tensor_scalar(fold[:, :], fold[:, :], gate[:, 0:1], None, ALU.mult).then_inc(folded, 1)

            with dve.Fori(1, B // 2) as i:
                for par in range(2):
                    dve.wait_ge(stat_in[par], i * 64)
                    take_stats(i * 2 + par, par)
            for par in range(2):
                dve.wait_ge(x_arrived, 64 * (par + 1))
                take_stats(par, par)
            dve.wait_ge(stat_taken, B)
            combine(0, stats[:, :, :, 0, :].rearrange("p b j (h s) -> p (b j) h s", s=3), C // 2)

            def prep_out(g_no, slot, piece):
                dve.wait_ge(prep_filled, g_no * 5 + piece + 1)
                if piece == 1:
                    last = dve.tensor_copy(kt[slot][:, 0, 0:4 * TT], m_ps[:, 0:4 * TT])
                else:
                    last = dve.tensor_copy(kt[slot][:, :, 4 * TT:T],
                                           m_ps[:, 0:4 * TT].rearrange("p (s t) -> p s t", s=2))
                last.then_inc(prep_dve, 1)

            def mask_and_max(n, s, lag):
                dve.wait_ge(scored, n + 1)
                if lag:
                    dve.wait_ge(expd, n - 1)
                dve.sem_inc(dve_passed, 1)
                dve.tensor_tensor_reduce(out=neg_scores[s % 2][:, :], in0=s_ps[s % 2][:, 0:T],
                                         in1=mask_sb[:, s % NJ, :], scale=-1.0, scalar=3.0e38, op0=ALU.add,
                                         op1=ALU.min, accum_out=neg_max[:, s:s + 1]).then_inc(masked, 1)

            def lo_parts(g_no, j):
                n = g_no * NJ + j
                c = int(j >= CH[0])
                for half in range(2):
                    dve.wait_ge(hi_out[half], n + 1)
                    at = (slice(None), j - c * CH[0], slice(half * HALF, (half + 1) * HALF), slice(None))
                    dve.tensor_tensor(pt_lo[c][at], pt_ps[half][0:TT, 0:HALF * P].rearrange("p (t c) -> p t c", c=P),
                                      pt_hi[c][at].bitcast(F32), ALU.subtract).then_inc(lo_out[half], 1)

            def normalize(g_no, slot, lag):
                dve.wait_ge(summed, g_no + 1)
                dve.reciprocal(row_inv[:, :], row_sum[:, slot, :]).then_inc(inverted, 1)
                dve.wait_ge(inverted, g_no + 1)
                if lag:
                    dve.wait_ge(added, g_no - 1)
                dve.tensor_tensor(att_n[slot][:, :, :], m_ps[:, 0:NJ * DH].rearrange("p (j d) -> p j d", d=DH),
                                  row_inv[:, :].unsqueeze(2).to_broadcast([P, NJ, DH]), ALU.mult).then_inc(normed, 1)

            def x1_stats(u):
                dve.wait_ge(added, u * 2 + 2)
                for j in range(NJ):
                    ins = dve.bn_stats(stats[:, (u >> 2) & (B - 1), j, u & 3, :], x1_pair[:, j, :, :].rearrange("p g d -> p (g d)"))
                ins.then_inc(x1_stat, 1)

            def x1t_out(u, lag):
                dve.wait_ge(xt_filled, u * 2 + 2)
                if lag:
                    dve.wait_ge(x1_stored, u * 32)
                dve.tensor_copy(x1t_sb[:, :, :, CH[0]:NJ].rearrange("p r q j -> p j (r q)"),
                                m_ps[:, 0:CH[1] * P].rearrange("p (j c) -> p j c", c=P)).then_inc(xt_dve, 1)

            def period(u, gg, new=True, lag=True, nxt=True, turn=True, first=False, second=False):
                g_no = u * 2 + gg
                for j in range(NJ):
                    n = g_no * NJ + j
                    if new:
                        mask_and_max(n, gg * NJ + j, lag or j >= 2)
                    if nxt and j in (1, 3):
                        prep_out(g_no + 1, 1 - gg, j)
                    if gg == 1 and turn and j == 2:
                        x1_stats(u - 1)
                    if gg == 1 and turn and j == 5:
                        x1t_out(u - 1, lag=not second)
                    if (j >= 2 and new) or (j < 2 and lag):
                        lo_parts(g_no - int(j < 2), (j - 2) % NJ)
                    if lag and j == 5:
                        normalize(g_no - 1, 1 - gg, lag=not (first or (second and gg == 0)))

            for piece in (1, 3):
                prep_out(0, 0, piece)
            dve.wait_ge(mask_in, 64)
            period(0, 0, lag=False, turn=False, first=True)
            period(0, 1, turn=False, first=True)
            period(1, 0, second=True)
            period(1, 1, second=True)
            with dve.Fori(2, PAIRS - 1) as u:
                period(u, 0)
                period(u, 1)
            period(PAIRS - 1, 0)
            period(PAIRS - 1, 1, nxt=False)
            period(PAIRS, 0, new=False, nxt=False, turn=False)
            x1_stats(PAIRS - 1)
            x1t_out(PAIRS - 1, True)
            dve.wait_ge(x1_stat, PAIRS)
            combine(1, stats[:, :, :, :, :].rearrange("p b j n (h s) -> p (b j) (n h) s", s=3), DH)



def feed_forward(nc, up, down, perm, consts, x1t_dram, stat_dram, zt_dram):
    gate = consts["gate"]
    UNITS = H * NC
    WCOLS = 2 * M
    with ExitStack() as es:
        def sb(name, shape, dt=F32):
            return es.enter_context(nc.sbuf_tensor(name, shape, dt))

        def sem(name):
            return es.enter_context(nc.semaphore(name))

        perm_sb = sb("perm_sb", [P, H], I32)
        rows_of = [sb(f"rows_of{i}", [P, 1], I32) for i in range(2)]
        mean_w = sb("mean_w", [P, ROWS])
        rstd_w = sb("rstd_w", [P, ROWS])
        xg = [sb(f"xg{i}", [P, ROWS]) for i in range(2)]
        w_raw = [sb(f"w_raw{i}", [P, WCOLS]) for i in range(2)]
        w_hi = [sb(f"w_hi{i}", [P, WCOLS], F32R) for i in range(2)]
        w_lo = [sb(f"w_lo{i}", [P, WCOLS], F32R) for i in range(2)]
        centered = sb("centered", [P, COLS])
        xnorm = [sb(f"xnorm{i}", [P, COLS]) for i in range(2)]
        x_hi = [sb(f"x_hi{i}", [P, COLS], F32R) for i in range(2)]
        x_lo = [sb(f"x_lo{i}", [P, COLS], F32R) for i in range(2)]
        hid = [sb(f"hid{i}", [P, MC, COLS]) for i in range(2)]
        hid_hi = [sb(f"hid_hi{i}", [P, MC, COLS], F32R) for i in range(2)]
        hid_lo = [sb(f"hid_lo{i}", [P, MC, COLS], F32R) for i in range(2)]
        up_ps = [es.enter_context(nc.psum_tensor(f"up_ps{i}", [P, 2, 512], F32)) for i in range(2)]
        dn_ps = es.enter_context(nc.psum_tensor("dn_ps", [P, 512], F32))

        perm_in = sem("perm_in")
        stats_in = sem("stats_in")
        weights_in = [sem(f"weights_in{i}") for i in range(2)]
        rows_set = sem("rows_set")
        gathered = [sem(f"gathered{i}") for i in range(2)]
        scattered = [sem(f"scattered{i}") for i in range(2)]
        weights_cut = sem("weights_cut")
        x_centered = sem("x_centered")
        x_normed = sem("x_normed")
        x_cut = sem("x_cut")
        up_done = sem("up_done")
        gelu_done = sem("gelu_done")
        hid_hi_done = sem("hid_hi_done")
        hid_lo_done = sem("hid_lo_done")
        down_done = sem("down_done")
        z_done = sem("z_done")
        pool_passed = sem("ff_pool_passed")

        block = es.enter_context(nc.Block())

        def cols(c):
            return bass.ds(c * COLS, COLS)

        def run(eng, unit):
            def pair(hp, first=False):
                for hh in range(2):
                    head = hp * 2 + hh
                    unit(head, hh, 0, first and hh == 0)
                    unit(head, hh, 1, first and hh == 0)
                    with eng.Fori(1, NC // 2) as cc:
                        unit(head, hh, cc * 2, False, even=True)
                        unit(head, hh, cc * 2 + 1, False, even=False)
            pair(0, first=True)
            with eng.Fori(1, H // 2) as hp:
                pair(hp)

        @block.sync
        def _(sp):
            sp.dma_start(perm_sb[:, :], perm.rearrange("(h p) -> p h", p=P), allow_slow_non_contiguous=True).then_inc(perm_in, 16)
            sp.dma_start(mean_w[:, :], stat_dram[0].partition_broadcast(P)).then_inc(stats_in, 16)
            sp.dma_start(rstd_w[:, :], stat_dram[1].partition_broadcast(P)).then_inc(stats_in, 16)

            def load_weights(head, hh):
                sp.dma_start(w_raw[hh][:, 0:M], up[head]).then_inc(weights_in[hh], 16)
                sp.dma_start(w_raw[hh][:, M:WCOLS].rearrange("p (m d) -> p m d", m=MC),
                             down[head].rearrange("(m p) d -> p m d", p=P)).then_inc(weights_in[hh], 16)

            load_weights(0, 0)
            load_weights(1, 1)
            with sp.Fori(1, H // 2) as hp:
                for hh in range(2):
                    sp.wait_ge(weights_cut, hp * 4 - 2 + 2 * hh)
                    load_weights(hp * 2 + hh, hh)

        @block.gpsimd
        def _(pool):
            pool.wait_ge(perm_in, 16)

            def gather(head, hh):
                pool.sem_inc(pool_passed, 1)
                pool.tensor_copy(rows_of[hh][:, :], perm_sb[:, bass.ds(head, 1)]).then_inc(rows_set, 1)
                pool.wait_ge(rows_set, head + 1)
                pool.sem_inc(pool_passed, 1)
                pool.indirect_dma_start(
                    out=xg[hh][:, :], out_offset=None, in_=x1t_dram,
                    in_offset=bass.IndirectOffsetOnAxis(ap=rows_of[hh][:, :].bitcast(U32), axis=0),
                ).then_inc(gathered[hh], 16)

            def scatter(head, hh):
                pool.wait_ge(z_done, (head + 1) * NC)
                pool.sem_inc(pool_passed, 1)
                pool.indirect_dma_start(
                    out=zt_dram, out_offset=bass.IndirectOffsetOnAxis(ap=rows_of[hh][:, :].bitcast(U32), axis=0),
                    in_=xg[hh][:, :], in_offset=None,
                ).then_inc(scattered[hh], 16)

            def cut_weights(head, hh, lag):
                pool.wait_ge(weights_in[hh], ((head >> 1) + 1) * 32)
                if lag:
                    pool.wait_ge(down_done, (head - 1) * NC)
                pool.sem_inc(pool_passed, 1)
                pool.tensor_copy(w_hi[hh][:, :], w_raw[hh][:, :]).then_inc(weights_cut, 1)
                pool.wait_ge(weights_cut, head * 2 + 1)
                pool.sem_inc(pool_passed, 1)
                pool.tensor_tensor(w_lo[hh][:, :], w_raw[hh][:, :], w_hi[hh][:, :].bitcast(F32),
                                   ALU.subtract).then_inc(weights_cut, 1)

            def normalize(head, hh, c, k, par, lag):
                pool.wait_ge(gathered[hh], ((head >> 1) + 1) * 16)
                if lag or c >= 1:
                    pool.wait_ge(x_normed, k)
                pool.sem_inc(pool_passed, 1)
                pool.tensor_tensor(centered[:, :], xg[hh][:, cols(c)], mean_w[:, cols(c)],
                                   ALU.subtract).then_inc(x_centered, 1)
                pool.wait_ge(x_centered, k + 1)
                if lag or c >= 2:
                    pool.wait_ge(x_cut, k * 2 - 2)
                pool.sem_inc(pool_passed, 1)
                pool.tensor_tensor(xnorm[par][:, :], centered[:, :], rstd_w[:, cols(c)],
                                   ALU.mult).then_inc(x_normed, 1)

            pool.wait_ge(stats_in, 32)
            gather(0, 0)
            gather(1, 1)
            cut_weights(0, 0, lag=False)

            def head_units(head, hh, first=False, last=False):
                k = head * NC
                for c in range(3):
                    normalize(head, hh, c, k + c, c % 2, lag=not first)
                if not last:
                    cut_weights(head + 1, 1 - hh, lag=not first)
                if not first:
                    scatter(head - 1, 1 - hh)
                for c in range(3, 6):
                    normalize(head, hh, c, k + c, c % 2, lag=True)
                if not first and not last:
                    pool.wait_ge(scattered[1 - hh], ((head + 1) >> 1) * 16)
                    gather(head + 1, 1 - hh)
                for c in range(6, NC):
                    normalize(head, hh, c, k + c, c % 2, lag=True)

            head_units(0, 0, first=True)
            head_units(1, 1)
            with pool.Fori(1, H // 2 - 1) as hp:
                head_units(hp * 2, 0)
                head_units(hp * 2 + 1, 1)
            head_units(H - 2, 0)
            head_units(H - 1, 1, last=True)
            scatter(H - 1, 1)
            pool.wait_ge(scattered[0], 16 * (H // 2))
            pool.wait_ge(scattered[1], 16 * (H // 2))

        @block.tensor
        def _(pe):
            def go_up(hh, k, par, new_head, lag):
                if new_head:
                    pe.wait_ge(weights_cut, (k >> 3) * 2 + 2)
                pe.wait_ge(x_cut, k * 2 + 2)
                for half in range(2):
                    if lag:
                        pe.wait_ge(gelu_done, k * 2 - 1 + half)
                    for i in range(2):
                        m = half * 2 + i
                        dst = up_ps[half][:, i, 0:COLS]
                        pe.matmul(dst, w_hi[hh][:, m * P:(m + 1) * P], x_hi[par][:, :], start=True, stop=False)
                        pe.matmul(dst, w_hi[hh][:, m * P:(m + 1) * P], x_lo[par][:, :], start=False, stop=False)
                        last = pe.matmul(dst, w_lo[hh][:, m * P:(m + 1) * P], x_hi[par][:, :], start=False, stop=True)
                    last.then_inc(up_done, 1)

            def go_down(hh, k, par, lag):
                pe.wait_ge(hid_lo_done, k * 2 + 2)
                if lag:
                    pe.wait_ge(z_done, k)
                for m in range(MC):
                    w = slice(M + m * P, M + (m + 1) * P)
                    pe.matmul(dn_ps[:, 0:COLS], w_hi[hh][:, w], hid_hi[par][:, m, :], start=(m == 0), stop=False)
                    pe.matmul(dn_ps[:, 0:COLS], w_hi[hh][:, w], hid_lo[par][:, m, :], start=False, stop=False)
                    last = pe.matmul(dn_ps[:, 0:COLS], w_lo[hh][:, w], hid_hi[par][:, m, :], start=False,
                                     stop=(m == MC - 1))
                last.then_inc(down_done, 1)

            def unit(head, hh, c, first, even=None):
                k = head * NC + c
                par = c % 2 if even is None else int(not even)
                go_up(hh, k, par, even is None and c == 0, lag=not (first and c == 0))
                if not (first and c == 0):
                    go_down(1 - hh if even is None and c == 0 else hh, k - 1, 1 - par, lag=not (first and c == 1))

            run(pe, unit)
            go_down(1, UNITS - 1, 1, lag=True)

        @block.scalar
        def _(act):
            def unit(head, hh, c, first, even=None):
                k = head * NC + c
                par = c % 2 if even is None else int(not even)
                for half in range(2):
                    at = slice(half * 2, half * 2 + 2)
                    act.wait_ge(up_done, k * 2 + half + 1)
                    if not first:
                        act.wait_ge(hid_lo_done, k * 2 - 3 + half)
                    act.activation(hid[par][:, at, :], up_ps[half][:, :, 0:COLS], ACT.Gelu).then_inc(gelu_done, 1)
                for half in range(2):
                    at = slice(half * 2, half * 2 + 2)
                    act.wait_ge(gelu_done, k * 2 + half + 1)
                    if not first:
                        act.wait_ge(down_done, k - 1)
                    act.activation(hid_hi[par][:, at, :], hid[par][:, at, :], ACT.Copy).then_inc(hid_hi_done, 1)

            run(act, unit)

        @block.vector
        def _(dve):
            def cut_x(k, par, first):
                dve.wait_ge(x_normed, k + 1)
                if not first:
                    dve.wait_ge(up_done, k * 2 - 2)
                dve.tensor_copy(x_hi[par][:, :], xnorm[par][:, :]).then_inc(x_cut, 1)
                dve.wait_ge(x_cut, k * 2 + 1)
                dve.tensor_tensor(x_lo[par][:, :], xnorm[par][:, :], x_hi[par][:, :].bitcast(F32),
                                  ALU.subtract).then_inc(x_cut, 1)

            def cut_hidden(k, par):
                for half in range(2):
                    at = slice(half * 2, half * 2 + 2)
                    dve.wait_ge(hid_hi_done, k * 2 + half + 1)
                    dve.tensor_tensor(hid_lo[par][:, at, :], hid[par][:, at, :], hid_hi[par][:, at, :].bitcast(F32),
                                      ALU.subtract).then_inc(hid_lo_done, 1)

            def result(hh, c, k):
                dve.wait_ge(down_done, k + 1)
                dve.scalar_tensor_tensor(out=xg[hh][:, cols(c)], in0=dn_ps[:, 0:COLS], scalar=gate[:, 1:2],
                                         in1=xg[hh][:, cols(c)], op0=ALU.mult, op1=ALU.add).then_inc(z_done, 1)

            def unit(head, hh, c, first, even=None):
                k = head * NC + c
                par = c % 2 if even is None else int(not even)
                cut_x(k, par, first)
                if not (first and c == 0):
                    cut_hidden(k - 1, 1 - par)
                if not first:
                    back = even is None
                    result(1 - hh if back else hh, c + NC - 2 if back else c - 2, k - 2)

            run(dve, unit)
            cut_hidden(UNITS - 1, 1)
            result(1, NC - 2, UNITS - 2)
            result(1, NC - 1, UNITS - 1)


def transpose_back(nc, consts, zt_dram, out):
    ident = consts["ident"]
    RING = 4
    TILES = ROWS // P
    F = D // P
    zt_view = zt_dram.rearrange("(f p) c -> p f c", p=P)
    out_view = out.rearrange("b q d -> (b q) d")
    with ExitStack() as es:
        z_in = [es.enter_context(nc.sbuf_tensor(f"z_in{i}", [P, F, P], F32)) for i in range(RING)]
        z_out = [es.enter_context(nc.sbuf_tensor(f"z_out{i}", [P, D], F32)) for i in range(RING)]
        z_ps = [es.enter_context(nc.psum_tensor(f"z_ps{i}", [P, D], F32)) for i in range(2)]
        loaded = [es.enter_context(nc.semaphore(f"loaded{i}")) for i in range(RING)]
        stored = [es.enter_context(nc.semaphore(f"stored{i}")) for i in range(RING)]
        turned = es.enter_context(nc.semaphore("z_turned"))
        act_out = es.enter_context(nc.semaphore("z_act_out"))
        dve_out = es.enter_context(nc.semaphore("z_dve_out"))
        block = es.enter_context(nc.Block())

        def ring(eng, tile):
            for s in range(RING):
                tile(s, s, 0, True)
            with eng.Fori(1, TILES // RING) as i:
                for s in range(RING):
                    tile(i * RING + s, s, i, False)

        @block.sync
        def _(sp):
            def tile(i, s, turn, first):
                if not first:
                    sp.wait_ge(turned, i - RING + 1)
                sp.dma_start(z_in[s][:, :, :], zt_view[:, :, bass.ds(i * P, P)]).then_inc(loaded[s], 16)

            ring(sp, tile)

        @block.tensor
        def _(pe):
            def tile(i, s, turn, first):
                pe.wait_ge(loaded[s], turn * 16 + 16)
                if not first or s >= 2:
                    pe.wait_ge(act_out, i - 1)
                    pe.wait_ge(dve_out, i - 1)
                for f in range(F):
                    last = pe.transpose(z_ps[s % 2][:, f * P:(f + 1) * P], z_in[s][:, f, :], ident[:, :])
                last.then_inc(turned, 1)

            ring(pe, tile)

        @block.scalar
        def _(act):
            def tile(i, s, turn, first):
                act.wait_ge(turned, i + 1)
                if not first:
                    act.wait_ge(stored[s], turn * 16)
                act.activation(z_out[s][:, 0:D // 2], z_ps[s % 2][:, 0:D // 2], ACT.Copy).then_inc(act_out, 1)
                act.wait_ge(act_out, i + 1)
                act.wait_ge(dve_out, i + 1)
                act.dma_start(out_view[bass.ds(i * P, P)], z_out[s][:, :]).then_inc(stored[s], 16)

            ring(act, tile)
            for s in range(RING):
                act.wait_ge(stored[s], TILES // RING * 16)

        @block.vector
        def _(dve):
            def tile(i, s, turn, first):
                dve.wait_ge(turned, i + 1)
                if not first:
                    dve.wait_ge(stored[s], turn * 16)
                dve.tensor_copy(z_out[s][:, D // 2:D], z_ps[s % 2][:, D // 2:D]).then_inc(dve_out, 1)

            ring(dve, tile)


_INS = ["x", "ctx_1024", "mask_SxS2_ff0", "g_xattn", "g_ffn", "L0_ffn_up", "L0_ffn_down", "L0_ffn_perm"]
_OUTS = [((B, SQ, D), "float32")]


def kernel(**inputs):
    import numpy as _np
    import concourse.bacc as _bacc
    from concourse import mybir as _mybir
    from concourse.bass_utils import run_bass_kernel_spmd as _run

    nc = _bacc.Bacc("TRN2", target_bir_lowering=False, num_devices=1)
    arrays, args = {}, []
    for name in _INS:
        a = _np.ascontiguousarray(inputs[name])
        arrays[f"in_{name}_dram"] = a
        args.append(nc.dram_tensor(f"in_{name}_dram", a.shape, _mybir.dt.from_np(a.dtype), kind="ExternalInput").ap())
    for i, (shape, dtype) in enumerate(_OUTS):
        dt = _mybir.dt.from_np(_np.dtype(dtype))
        args.append(nc.dram_tensor(f"out_{i}_dram", shape, dt, kind="ExternalOutput").ap())
    build(nc, *args)
    r = _run(nc, [arrays], core_ids=[0])
    return r.results[0]["out_0_dram"]
```

```python
from contextlib import ExitStack

import concourse.bass as bass
from concourse import mybir

F32 = mybir.dt.float32
F32R = mybir.dt.float32r
I32 = mybir.dt.int32
U32 = mybir.dt.uint32
ALU = mybir.AluOpType
ACT = mybir.ActivationFunctionType
AX_X = mybir.AxisListType.X

P = 128
B, SQ, D = 16, 224, 2048
T, C = 750, 512
NG, NR, DH = 8, 4, 64
ROWS = B * SQ
PJ = P // NR
NJ = SQ // PJ
NT, TT = 6, T // 6
NPAIR = NG // 2
PAIRS = B * NPAIR
CH = (4, 3)
QW = NJ * P
EPS = 1e-5
STEPS = 7
HALF = NT // 2
GROUPS = B * NG
TILES = GROUPS * NJ
PER_BATCH = NPAIR - 1
JS, JSTEP = 3, 2
NSTEPS = 8
H, M = 16, 512
MC = M // P
COLS, NC = 448, 8
SCALE = float(DH)


def await_(eng, semaphore, count):
    if not isinstance(count, int) or count > 0:
        eng.wait_ge(semaphore, count)


def exists(number, end):
    return not isinstance(number, int) or 0 <= number < end


def build(nc, x, ctx_in, mask, g_x, g_f, up, down, perm, out):
    x1t_dram = nc.dram_tensor("x1t_scratch", [D, ROWS], F32).ap()
    zt_dram = nc.dram_tensor("zt_scratch", [D, ROWS], F32).ap()
    stat_dram = nc.dram_tensor("stat_scratch", [2, ROWS], F32).ap()

    with ExitStack() as keep:
        consts = {
            "ident": keep.enter_context(nc.sbuf_tensor("ident", [P, P], F32)),
            "gate": keep.enter_context(nc.sbuf_tensor("gate", [P, 2], F32)),
        }
        attention(nc, x, ctx_in, mask, g_x, g_f, consts, x1t_dram, stat_dram)
        feed_forward(nc, up, down, perm, consts, x1t_dram, stat_dram, zt_dram)
        transpose_back(nc, consts, zt_dram, out)


def attention(nc, x, ctx_in, mask, g_x, g_f, consts, x1t_dram, stat_dram):
    ident, gate = consts["ident"], consts["gate"]
    x_view = x.rearrange("b (p j) (g r d) -> b r p j g d", j=NJ, g=NG, r=NR)
    ctx_view = ctx_in.rearrange("b (t p) c -> b p t c", p=TT)
    mask_view = mask.rearrange("(p j) t -> p j t", j=NJ)
    x1t_view = x1t_dram.rearrange("(n gg r d) c -> n gg d r c", n=NPAIR, gg=2, r=NR)
    stat_view = stat_dram.rearrange("s (b p j) -> s p b j", b=B, j=NJ)

    with ExitStack() as es:
        def sb(name, shape, dt=F32):
            return es.enter_context(nc.sbuf_tensor(name, shape, dt))

        def ps(name, cols):
            return es.enter_context(nc.psum_tensor(name, [P, cols], F32))

        def sem(name):
            return es.enter_context(nc.semaphore(name))

        mask_sb = sb("mask_sb", [P, NJ, T])
        x_raw = sb("x_raw", [P, 2, NJ, NG, DH])
        ctx_sb = sb("ctx_sb", [TT, 2, NT, C])
        k_split = [sb(f"k_split{i}", [TT, NT, 4, DH], F32R) for i in range(2)]
        values = [sb(f"values{i}", [TT, NT, 2 * DH], F32R) for i in range(2)]
        q_split = sb("q_split", [P, NJ, 2 * DH], F32R)
        qt = [sb(f"qt{i}", [P, QW], F32R) for i in range(2)]
        kt = [sb(f"kt{i}", [P, 2, T], F32R) for i in range(2)]
        neg_scores = [sb(f"neg_scores{i}", [P, T]) for i in range(2)]
        probs = [sb(f"probs{i}", [P, T]) for i in range(2)]
        pt_hi = [sb(f"pt_hi{c}", [TT, CH[c], NT, P], F32R) for c in range(2)]
        pt_lo = [sb(f"pt_lo{c}", [TT, CH[c], NT, P], F32R) for c in range(2)]
        att_t = sb("att_t", [P, QW])
        att_n = [sb(f"att_n{i}", [P, NJ, DH]) for i in range(2)]
        x1_pair = sb("x1_pair", [P, NJ, 2, DH])
        x1t_sb = sb("x1t_sb", [P, NR, PJ, NJ])
        ident_r = sb("ident_r", [P, P], F32R)
        xn = sb("xn", [P, NJ, DH])
        neg_max = sb("neg_max", [P, 2 * NJ])
        row_sum = sb("row_sum", [P, 2, NJ])
        row_inv = sb("row_inv", [P, NJ])
        stats = sb("stats", [P, B, NJ, NPAIR, 6])
        mean = sb("mean", [P, B * NJ])
        rstd = sb("rstd", [P, B * NJ])
        var = sb("var", [P, B * NJ])
        part = sb("part", [P, B * NJ])
        next_triples = sb("next_triples", [P, JS, 2, 3])
        next_part = sb("next_part", [P, JS])
        next_var = sb("next_var", [P, JS])
        power = sb("power", [P, B * NJ])
        same = sb("same", [P, P])
        ones = sb("ones", [P, 1])
        fold = sb("fold", [P, DH])

        s_ps = [ps(f"s_ps{i}", 1024) for i in range(2)]
        pt_ps = [ps(f"pt_ps{i}", 512) for i in range(2)]
        sums_ps = pt_ps[1][:, HALF * P:HALF * P + JS]
        o_ps = ps("o_ps", 512)
        m_ps = ps("m_ps", 512)

        gates_in = sem("gates_in")
        mask_in = sem("mask_in")
        zeroed = sem("zeroed")
        marked = sem("marked")
        gated = sem("gated")
        folded = sem("folded")
        powered = sem("powered")
        stat_v = sem("stat_v")
        stat_taken = sem("stat_taken")
        stat_pe = sem("stat_pe")
        stat_done = sem("stat_done")
        next_stat = sem("next_stat")
        next_sum = sem("next_sum")
        next_rstd = sem("next_rstd")
        x_arrived = sem("x_arrived")
        ctx_arrived = sem("ctx_arrived")
        k_cut = sem("k_cut")
        q_cut = sem("q_cut")
        v_put = sem("v_put")
        prep_filled = sem("prep_filled")
        prep_act = sem("prep_act")
        prep_dve = sem("prep_dve")
        scored = sem("scored")
        masked = sem("masked")
        expd = sem("expd")
        turned = [sem(f"turned{i}") for i in range(2)]
        hi_out = [sem(f"hi_out{i}") for i in range(2)]
        lo_out = [sem(f"lo_out{i}") for i in range(2)]
        weighed = sem("weighed")
        att_out = sem("att_out")
        summed = sem("summed")
        inverted = sem("inverted")
        normed = sem("normed")
        added = sem("added")
        x1_stat = sem("x1_stat")
        xt_filled = sem("xt_filled")
        xt_dve = sem("xt_dve")
        x1_stored = sem("x1_stored")
        stat_stored = sem("stat_stored")
        dve_passed = sem("dve_passed")
        pool_passed = sem("pool_passed")
        sp_passed = sem("sp_passed")

        block = es.enter_context(nc.Block())

        def load_x(sp, b, par, s):
            for r in range(NR):
                sp.dma_start(x_raw[PJ * r:PJ * (r + 1), par], x_view[b, r]).then_inc(s, 16)

        def load_ctx(sp, b, par):
            sp.dma_start(ctx_sb[:, par], ctx_view[b]).then_inc(ctx_arrived, 16)

        @block.sync
        def _(sp):
            sp.dma_start(gate[:, 0:1], g_x.partition_broadcast(P)).then_inc(gates_in, 16)
            sp.dma_start(gate[:, 1:2], g_f.partition_broadcast(P)).then_inc(gates_in, 16)
            load_x(sp, 0, 0, x_arrived)
            load_ctx(sp, 0, 0)
            for r in range(NR):
                sp.dma_start(mask_sb[PJ * r:PJ * (r + 1)], mask_view).then_inc(mask_in, 16)
            sp.wait_ge(ctx_arrived, 16)
            load_ctx(sp, 1, 1)
            sp.wait_ge(x_arrived, 64)
            load_x(sp, 1, 1, x_arrived)

            def store_pair(b, n):
                u = b * NPAIR + n
                sp.wait_ge(xt_dve, u * 2 + 2)
                for gg in range(2):
                    sp.dma_start(x1t_view[n, gg][:, :, bass.ds(b * SQ, SQ)],
                                 x1t_sb[DH * gg:DH * (gg + 1)].rearrange("p r q j -> p r (q j)")
                                 ).then_inc(x1_stored, 16)

            def store_batch(b):
                with sp.Fori(0, NPAIR) as n:
                    store_pair(b, n)

            with sp.Fori(0, B // 2 - 1) as i:
                for par in range(2):
                    b = i * 2 + par
                    with sp.Fori(0, NPAIR - 1) as n:
                        store_pair(b, n)
                    sp.wait_ge(ctx_arrived, (b + 2) * 16)
                    sp.sem_inc(sp_passed, 1)
                    sp.wait_ge(k_cut, (b + 1) * (2 * NG))
                    load_ctx(sp, b + 2, par)
                    sp.wait_ge(x_arrived, (b + 2) * 64)
                    sp.sem_inc(sp_passed, 1)
                    sp.wait_ge(added, (b + 1) * NG)
                    load_x(sp, b + 2, par, x_arrived)
                    store_pair(b, NPAIR - 1)
            for par in range(2):
                store_batch(B - 2 + par)
            sp.wait_ge(x1_stored, 32 * PAIRS)
            sp.wait_ge(stat_v, 2 * STEPS)
            sp.wait_ge(stat_done, 2)
            for k, t in enumerate((mean, rstd)):
                sp.dma_start(stat_view[k], t[0:PJ, :].rearrange("p (b j) -> p b j", j=NJ)).then_inc(stat_stored, 16)
            sp.wait_ge(stat_stored, 32)

        def ctx_group(g_no):
            return ctx_sb[:, (g_no >> 3) & 1, :, bass.ds((g_no & 7) * DH, DH)]

        def x_group(g_no):
            return x_raw[:, (g_no >> 3) & 1, :, g_no & 7, :]

        def of_batch(t, g_no):
            return t[:, bass.ds(((g_no >> 3) & (B - 1)) * NJ, NJ)].unsqueeze(2).to_broadcast([P, NJ, DH])

        def all_periods(eng, period):
            def pair(u, stat=None):
                for gg in range(2):
                    period(u, gg, stat if gg == 0 else None)
            pair(0)
            pair(1, (1, 0, 0))
            with eng.Fori(2, NPAIR) as n:
                pair(n, (1, n - 1, n - 1))
            with eng.Fori(1, B - 1) as b:
                pair(b * NPAIR)
                with eng.Fori(1, NPAIR) as n:
                    pair(b * NPAIR + n, (b + 1, n - 1, b * PER_BATCH + n - 1))
            with eng.Fori(PAIRS - NPAIR, PAIRS - 1) as u:
                pair(u)
            pair(PAIRS - 1)
            pair(PAIRS)

        @block.gpsimd
        def _(pool):
            pool.memset(ident[:, :], 0.0).then_inc(zeroed, 1)
            pool.memset(same[:, :], 0.0).then_inc(zeroed, 1)
            pool.memset(power[:, :], -0.5).then_inc(powered, 1)
            pool.memset(ones[:, :], 1.0).then_inc(powered, 1)
            pool.wait_ge(zeroed, 2)
            pool.affine_select(out=ident[:, :], in_=ident[:, :], compare_op=ALU.not_equal, fill=1.0,
                               base=0, pattern=[[-1, P]], channel_multiplier=1).then_inc(marked, 1)
            for k in range(2 * NR - 1):
                pool.wait_ge(marked, k + 1)
                pool.affine_select(out=same[:, :], in_=same[:, :], compare_op=ALU.not_equal, fill=1.0,
                                   base=PJ * (k - NR + 1), pattern=[[-1, P]],
                                   channel_multiplier=1).then_inc(marked, 1)
            pool.tensor_copy(ident_r[:, :], ident[:, :]).then_inc(marked, 1)
            pool.wait_ge(powered, 2)

            def reciprocal_deviation(k, n):
                pool.wait_ge(stat_v, STEPS * (k + 1))
                pool.tensor_tensor(rstd[:, 0:n], var[:, 0:n], power[:, 0:n], ALU.pow).then_inc(stat_done, 1)

            def next_deviation(b, m, k):
                pool.wait_ge(next_stat, k * NSTEPS + NSTEPS)
                pool.sem_inc(pool_passed, 1)
                pool.tensor_tensor(rstd[:, bass.ds(b * NJ + m, JS, JSTEP)], next_var[:, :],
                                   power[:, 0:JS], ALU.pow).then_inc(next_rstd, 1)

            def cut_context(g_no, slot):
                pool.wait_ge(ctx_arrived, ((g_no >> 3) + 1) * 16)
                await_(pool, prep_filled, g_no * 5 - 7)
                await_(pool, v_put, g_no - 1)
                src = ctx_group(g_no).unsqueeze(2).to_broadcast([TT, NT, 2, DH])
                pool.sem_inc(pool_passed, 1)
                pool.tensor_tensor(k_split[slot][:, :, 0:2, :], src,
                                   ones[0:TT, :].unsqueeze(2).unsqueeze(3).to_broadcast([TT, NT, 2, DH]),
                                   ALU.mult).then_inc(k_cut, 1)
                pool.wait_ge(k_cut, g_no * 2 + 1)
                pool.sem_inc(pool_passed, 1)
                pool.tensor_tensor(k_split[slot][:, :, 2:4, :], src, k_split[slot][:, :, 0:2, :].bitcast(F32),
                                   ALU.subtract).then_inc(k_cut, 1)

            def cut_queries(g_no):
                pool.wait_ge(x_arrived, ((g_no >> 3) + 1) * 64)
                await_(pool, next_rstd, (g_no >> 3) * PER_BATCH)
                await_(pool, prep_filled, g_no * 5)
                await_(pool, q_cut, g_no * 4)
                pool.sem_inc(pool_passed, 1)
                pool.tensor_tensor(xn[:, :, :], x_group(g_no), of_batch(mean, g_no), ALU.subtract).then_inc(q_cut, 1)
                pool.wait_ge(q_cut, g_no * 4 + 1)
                pool.sem_inc(pool_passed, 1)
                pool.tensor_tensor(xn[:, :, :], xn[:, :, :], of_batch(rstd, g_no), ALU.mult).then_inc(q_cut, 1)
                pool.wait_ge(q_cut, g_no * 4 + 2)
                pool.sem_inc(pool_passed, 1)
                pool.tensor_tensor(q_split[:, :, 0:DH], xn[:, :, :],
                                   ones[:, :].unsqueeze(2).to_broadcast([P, NJ, DH]), ALU.mult).then_inc(q_cut, 1)
                pool.wait_ge(q_cut, g_no * 4 + 3)
                pool.sem_inc(pool_passed, 1)
                pool.tensor_tensor(q_split[:, :, DH:2 * DH], xn[:, :, :], q_split[:, :, 0:DH].bitcast(F32),
                                   ALU.subtract).then_inc(q_cut, 1)

            def put_values(g_no, slot):
                pool.wait_ge(k_cut, g_no * 2 + 2)
                await_(pool, weighed, g_no * 2 - 2)
                pool.sem_inc(pool_passed, 1)
                src = k_split[slot][:, :, 1:3, :].rearrange("p t s d -> p t (s d)").bitcast(F32)
                pool.tensor_tensor(values[slot][:, :, :], src,
                                   ones[0:TT, :].unsqueeze(2).to_broadcast([TT, NT, 2 * DH]),
                                   ALU.mult).then_inc(v_put, 1)

            def add_x(g_no, gg):
                pool.wait_ge(normed, g_no + 1)
                if gg == 0:
                    await_(pool, xt_filled, g_no)
                    await_(pool, x1_stat, g_no >> 1)
                pool.sem_inc(pool_passed, 1)
                pool.tensor_tensor(x1_pair[:, :, gg, :], att_n[gg][:, :, :], x_group(g_no),
                                   ALU.add).then_inc(added, 1)

            def period(u, gg, stat):
                g_no = u * 2 + gg
                if exists(g_no + 1, GROUPS):
                    cut_queries(g_no + 1)
                if exists(g_no + 2, GROUPS):
                    cut_context(g_no + 2, gg)
                if exists(g_no + 1, GROUPS):
                    put_values(g_no + 1, 1 - gg)
                if exists(g_no - 1, GROUPS):
                    add_x(g_no - 1, 1 - gg)
                if stat:
                    next_deviation(*stat)

            reciprocal_deviation(0, NJ)
            pool.wait_ge(stat_done, 1)
            cut_queries(0)
            cut_context(0, 0)
            cut_context(1, 1)
            put_values(0, 0)
            all_periods(pool, period)
            reciprocal_deviation(1, B * NJ)

        @block.tensor
        def _(pe):
            def sum_partitions(k, n):
                for step in range(2):
                    pe.wait_ge(stat_v, STEPS * k + (1, 6)[step])
                    if k == 0 and step == 0:
                        pe.wait_ge(marked, 2 * NR + 1)
                    if k == 1 and step == 0:
                        pe.wait_ge(xt_dve, 2 * PAIRS)
                    pe.matmul(m_ps[:, 0:n], same[:, :], part[:, 0:n], start=True, stop=True).then_inc(stat_pe, 1)

            def sum_next(k, step):
                pe.wait_ge(next_stat, k * NSTEPS + (2, 7)[step])
                pe.matmul(sums_ps, same[:, :], next_part[:, :], start=True, stop=True).then_inc(next_sum, 1)

            def turn_keys(slot, col, t, part_no):
                src = k_split[slot][:, t, 2 * part_no:2 * part_no + 2, :].rearrange("p s d -> p (s d)")
                return pe.matmul(m_ps[:, col * (TT + 1):(col + 1) * (TT + 1)], src, ident_r[0:TT, 0:TT + 1],
                                 start=True, stop=True)

            def prep(g_no, slot, piece, free, count):
                if piece == 0:
                    pe.wait_ge(k_cut, g_no * 2 + 2)
                if piece == 3:
                    pe.wait_ge(q_cut, g_no * 4 + 4)
                await_(pe, free, count)
                if piece < 2:
                    for t in range(4):
                        last = turn_keys(slot, t, t, piece)
                elif piece == 2:
                    for k in range(4):
                        last = turn_keys(slot, k, 4 + k % 2, k // 2)
                else:
                    j0 = (0, CH[0])[piece - 3]
                    for j in range(CH[piece - 3]):
                        last = pe.matmul(m_ps[:, j * P:(j + 1) * P], q_split[:, j0 + j, :], ident_r[:, :],
                                         start=True, stop=True)
                last.then_inc(prep_filled, 1)

            def scores(g_no, slot, j):
                n = g_no * NJ + j
                buf = (slot * NJ + j) % 2
                if j == 0:
                    pe.wait_ge(prep_act, g_no * 4 + 3)
                    pe.wait_ge(prep_dve, g_no + 1)
                if j == CH[0]:
                    pe.wait_ge(prep_act, g_no * 4 + 4)
                await_(pe, masked, n - 1)
                q = qt[slot][:, j * P:(j + 1) * P]
                for c0, c1 in ((0, 512), (512, T)):
                    pe.matmul(s_ps[buf][:, c0:c1], q, kt[slot][:, 0, c0:c1], start=True, stop=False)
                    last = pe.matmul(s_ps[buf][:, c0:c1], q, kt[slot][:, 1, c0:c1], start=False, stop=True)
                last.then_inc(scored, 1)

            def turn_probs(n, buf, sums=None):
                pe.wait_ge(expd, n + 1)
                for half in range(2):
                    await_(pe, lo_out[half], n)
                    if sums and half == 1:
                        sum_next(*sums)
                    for k in range(HALF):
                        t = half * HALF + k
                        last = pe.transpose(pt_ps[half][0:TT, k * P:(k + 1) * P],
                                            probs[buf][:, t * TT:(t + 1) * TT], ident[:, :])
                    last.then_inc(turned[half], 1)

            def weigh(g_no, slot, c, third):
                width = CH[c] * P
                if third == 0:
                    pe.wait_ge(lo_out[1], g_no * NJ + (CH[0], NJ)[c])
                    if c == 0:
                        pe.wait_ge(v_put, g_no + 1)
                        await_(pe, normed, g_no)
                    else:
                        pe.wait_ge(att_out, g_no * 2 + 1)
                for t in (2 * third, 2 * third + 1):
                    for k, src in enumerate((pt_hi[c], pt_lo[c])):
                        last = pe.matmul(o_ps[:, 0:width], values[slot][:, t, :], src[:, :, t, :],
                                         start=(t == 0 and k == 0), stop=(t == NT - 1 and k == 1))
                if third == 2:
                    last.then_inc(weighed, 1)

            def fold_parts(g_no):
                pe.wait_ge(att_out, g_no * 2 + 2)
                pe.wait_ge(folded, 2)
                for j in range(NJ):
                    last = pe.matmul(o_ps[:, j * DH:(j + 1) * DH], att_t[:, j * P:(j + 1) * P], fold[:, :],
                                     start=True, stop=True)
                last.then_inc(summed, 1)

            def turn_x1(u, piece):
                if piece == 0:
                    pe.wait_ge(added, u * 2 + 2)
                for j in range(CH[piece]):
                    last = pe.transpose(m_ps[:, j * P:(j + 1) * P],
                                        x1_pair[:, (0, CH[0])[piece] + j, :, :].rearrange("p g d -> p (g d)"),
                                        ident[:, :])
                last.then_inc(xt_filled, 1)

            def period(u, gg, stat):
                g_no = u * 2 + gg
                nxt = exists(g_no + 1, GROUPS)
                nx = g_no + 1
                turn = gg == 1 and exists(u - 1, PAIRS)
                before = exists(g_no - 1, GROUPS)
                for j in range(NJ):
                    n = g_no * NJ + j
                    if exists(n, TILES):
                        scores(g_no, gg, j)
                    if nxt and j == 1 - gg:
                        prep(nx, 1 - gg, 0, prep_act, nx * 4)
                    if nxt and j == 2 - gg:
                        prep(nx, 1 - gg, 1, prep_act, nx * 4 + 1)
                    if turn and j == 2:
                        if nxt:
                            pe.wait_ge(prep_dve, nx + 1)
                        else:
                            pe.wait_ge(prep_act, GROUPS * 4)
                            pe.wait_ge(xt_dve, u * 2 - 2)
                        turn_x1(u - 1, 0)
                    if nxt and j == 3:
                        if turn:
                            prep(nx, 1 - gg, 2, xt_dve, u * 2 - 1)
                        else:
                            prep(nx, 1 - gg, 2, prep_dve, nx + 1)
                    if nxt and j == 4:
                        prep(nx, 1 - gg, 3, prep_act, nx * 4 + 2)
                    if turn and j == 5:
                        if nxt:
                            pe.wait_ge(prep_act, nx * 4 + 3)
                        else:
                            pe.wait_ge(xt_dve, u * 2 - 1)
                        turn_x1(u - 1, 1)
                    if nxt and j == 5 + gg:
                        if turn:
                            prep(nx, 1 - gg, 4, xt_dve, u * 2)
                        else:
                            prep(nx, 1 - gg, 4, prep_act, nx * 4 + 3)
                    if exists(n - 2, TILES):
                        turn_probs(n - 2, (gg * NJ + j) % 2,
                                   (stat[2], j // 2 - 2) if stat and j in (4, 6) else None)
                    if before and j < 2:
                        weigh(g_no - 1, 1 - gg, 0, j + 1)
                    if before and j in (2, 3, 4):
                        weigh(g_no - 1, 1 - gg, 1, j - 2)
                    if before and j == 5:
                        fold_parts(g_no - 1)
                    if exists(g_no, GROUPS) and j == 6:
                        weigh(g_no, gg, 0, 0)

            sum_partitions(0, NJ)
            pe.wait_ge(stat_v, STEPS)
            prep(0, 0, 0, prep_act, 0)
            prep(0, 0, 1, prep_act, 1)
            prep(0, 0, 2, prep_dve, 1)
            for piece in (3, 4):
                prep(0, 0, piece, prep_act, piece - 1)
            all_periods(pe, period)
            sum_partitions(1, B * NJ)

        @block.scalar
        def _(act):
            act.wait_ge(gates_in, 32)
            act.activation(gate[:, :], gate[:, :], ACT.Tanh).then_inc(gated, 1)

            def prep_out(g_no, slot, piece):
                act.wait_ge(prep_filled, g_no * 5 + piece + 1)
                blocks = m_ps[:, 0:4 * (TT + 1)].rearrange("p (t c) -> p t c", c=TT + 1)[:, :, 0:TT]
                if piece == 0:
                    last = act.activation(kt[slot][:, 0, 0:4 * TT].rearrange("p (t c) -> p t c", c=TT), blocks, ACT.Copy)
                elif piece == 2:
                    last = act.activation(kt[slot][:, :, 4 * TT:T].rearrange("p s (t c) -> p s t c", c=TT),
                                          blocks.rearrange("p (s t) c -> p s t c", s=2), ACT.Copy)
                elif piece == 3:
                    last = act.activation(qt[slot][:, 0:CH[0] * P], m_ps[:, 0:CH[0] * P], ACT.Copy)
                else:
                    last = act.activation(qt[slot][:, CH[0] * P:QW], m_ps[:, 0:CH[1] * P], ACT.Copy)
                last.then_inc(prep_act, 1)

            def exponentials(n, s):
                act.wait_ge(masked, n + 1)
                await_(act, turned[1], n - 1)
                act.activation(probs[s % 2][:, :], neg_scores[s % 2][:, :], ACT.Exp, bias=neg_max[:, s:s + 1],
                               scale=-1.0, accum_out=row_sum[:, s // NJ, s % NJ:s % NJ + 1]).then_inc(expd, 1)

            def hi_parts(g_no, j):
                n = g_no * NJ + j
                c = int(j >= CH[0])
                if j in (0, CH[0]):
                    await_(act, weighed, g_no * 2 - 1 + c)
                for half in range(2):
                    act.wait_ge(turned[half], n + 1)
                    act.activation(pt_hi[c][:, j - c * CH[0], half * HALF:(half + 1) * HALF, :],
                                   pt_ps[half][0:TT, 0:HALF * P], ACT.Copy).then_inc(hi_out[half], 1)

            def att_evacuate(g_no, c):
                act.wait_ge(weighed, g_no * 2 + c + 1)
                if c == 0:
                    await_(act, summed, g_no)
                act.activation(att_t[:, c * CH[0] * P:(c * CH[0] + CH[c]) * P], o_ps[:, 0:CH[c] * P],
                               ACT.Copy).then_inc(att_out, 1)

            def period(u, gg, stat):
                g_no = u * 2 + gg
                for j in range(NJ):
                    n = g_no * NJ + j
                    if exists(n - 1, TILES):
                        exponentials(n - 1, (gg * NJ + j - 1) % (2 * NJ))
                    if exists(g_no - 1, GROUPS) and j in (2, 5):
                        att_evacuate(g_no - 1, j // 3)
                    if exists(g_no + 1, GROUPS) and j in (1 - gg, 3, 4, 5 + gg):
                        prep_out(g_no + 1, 1 - gg, {1 - gg: 0, 3: 2, 4: 3, 5 + gg: 4}[j])
                    if exists(n - 2, TILES):
                        hi_parts(g_no - int(j < 2), (j - 2) % NJ)

            for piece in (0, 2, 3, 4):
                prep_out(0, 0, piece)
            all_periods(act, period)

        @block.vector
        def _(dve):
            def combine(triples, count, n, mean_of, part_of, var_of, chain, base, sums, sums_base, scale,
                        summed_ps):
                n_parts = D // count
                mu = triples[:, :, :, 1]
                mean_wide = mean_of.unsqueeze(2).to_broadcast([P, n, n_parts // NR])
                dve.tensor_reduce(part_of, mu, AX_X, ALU.add).then_inc(chain, 1)
                yield
                dve.wait_ge(sums, sums_base + 1)
                dve.tensor_scalar(mean_of, summed_ps, 1.0 / n_parts, None, ALU.mult).then_inc(chain, 1)
                yield
                dve.wait_ge(chain, base + 2)
                dve.tensor_tensor(mu, mu, mean_wide, ALU.subtract).then_inc(chain, 1)
                dve.wait_ge(chain, base + 3)
                dve.tensor_tensor(mu, mu, mu, ALU.mult).then_inc(chain, 1)
                dve.wait_ge(chain, base + 4)
                dve.scalar_tensor_tensor(out=mu, in0=mu, scalar=float(count), in1=triples[:, :, :, 2],
                                         op0=ALU.mult, op1=ALU.add).then_inc(chain, 1)
                dve.wait_ge(chain, base + 5)
                dve.tensor_reduce(part_of, mu, AX_X, ALU.add).then_inc(chain, 1)
                yield
                dve.wait_ge(sums, sums_base + 2)
                dve.tensor_scalar(var_of, summed_ps, scale / D, EPS * scale, ALU.mult, ALU.add).then_inc(chain, 1)
                yield

            def take_stats(dst, tile):
                return dve.bn_stats(dst, tile.rearrange("p g d -> p (g d)"))

            dve.wait_ge(marked, 2 * NR)
            dve.tensor_tensor(fold[:, :], ident[:, 0:DH], ident[:, DH:P], ALU.add).then_inc(folded, 1)
            dve.wait_ge(gated, 1)
            dve.wait_ge(folded, 1)
            dve.tensor_scalar(fold[:, :], fold[:, :], gate[:, 0:1], None, ALU.mult).then_inc(folded, 1)

            dve.wait_ge(x_arrived, 64)
            for j in range(NJ):
                ins = take_stats(stats[:, 0, j, 0, :], x_raw[:, 0, j])
            ins.then_inc(stat_taken, 1)
            dve.wait_ge(stat_taken, 1)
            for _ in combine(stats[:, 0, :, 0, :].rearrange("p j (h s) -> p j h s", s=3), C // 2, NJ,
                             mean[:, 0:NJ], part[:, 0:NJ], var[:, 0:NJ], stat_v, 0, stat_pe, 0, SCALE,
                             m_ps[:, 0:NJ]):
                pass

            def next_norm(b, m, k):
                dve.wait_ge(x_arrived, b * 64 + 64)
                await_(dve, next_rstd, k)
                for i in range(JS):
                    ins = take_stats(next_triples[:, i].rearrange("p h s -> p (h s)"),
                                     x_raw[:, b & 1, bass.ds(m + i * JSTEP, 1)].rearrange("p j g d -> p (j g) d"))
                    if i == JS - 1:
                        ins.then_inc(next_stat, 1)
                    else:
                        yield
                dve.wait_ge(next_stat, k * NSTEPS + 1)
                yield from combine(next_triples[:, :], C // 2, JS, mean[:, bass.ds(b * NJ + m, JS, JSTEP)],
                                   next_part[:, :], next_var[:, :], next_stat, k * NSTEPS + 1, next_sum, k * 2,
                                   SCALE, sums_ps)

            def prep_out(g_no, slot):
                dve.wait_ge(prep_filled, g_no * 5 + 2)
                dve.tensor_copy(kt[slot][:, 1, 0:4 * TT].rearrange("p (t c) -> p t c", c=TT),
                                m_ps[:, 0:4 * (TT + 1)].rearrange("p (t c) -> p t c", c=TT + 1)[:, :, 0:TT]
                                ).then_inc(prep_dve, 1)

            def mask_and_max(n, s):
                dve.wait_ge(scored, n + 1)
                await_(dve, expd, n - 1)
                dve.sem_inc(dve_passed, 1)
                dve.tensor_tensor_reduce(out=neg_scores[s % 2][:, :], in0=s_ps[s % 2][:, 0:T],
                                         in1=mask_sb[:, s % NJ, :], scale=-1.0, scalar=3.0e38, op0=ALU.add,
                                         op1=ALU.min, accum_out=neg_max[:, s:s + 1]).then_inc(masked, 1)

            def lo_parts(g_no, j, norm=None):
                n = g_no * NJ + j
                c = int(j >= CH[0])
                for half in range(2):
                    dve.wait_ge(hi_out[half], n + 1)
                    if norm and half == 1:
                        next(norm)
                    at = (slice(None), j - c * CH[0], slice(half * HALF, (half + 1) * HALF), slice(None))
                    dve.tensor_tensor(pt_lo[c][at], pt_ps[half][0:TT, 0:HALF * P].rearrange("p (t c) -> p t c", c=P),
                                      pt_hi[c][at].bitcast(F32), ALU.subtract).then_inc(lo_out[half], 1)

            def normalize(g_no, slot):
                dve.wait_ge(summed, g_no + 1)
                dve.reciprocal(row_inv[:, :], row_sum[:, slot, :]).then_inc(inverted, 1)
                dve.wait_ge(inverted, g_no + 1)
                await_(dve, added, g_no - 1)
                dve.tensor_tensor(att_n[slot][:, :, :], o_ps[:, 0:NJ * DH].rearrange("p (j d) -> p j d", d=DH),
                                  row_inv[:, :].unsqueeze(2).to_broadcast([P, NJ, DH]), ALU.mult).then_inc(normed, 1)

            def x1_stats(u, tiles):
                if 0 in tiles:
                    dve.wait_ge(added, u * 2 + 2)
                for j in tiles:
                    ins = take_stats(stats[:, (u >> 2) & (B - 1), j, u & 3, :], x1_pair[:, j])
                if NJ - 1 in tiles:
                    ins.then_inc(x1_stat, 1)

            def x1t_out(u, c):
                dve.wait_ge(xt_filled, u * 2 + c + 1)
                if c == 0:
                    await_(dve, x1_stored, u * 32)
                dve.tensor_copy(x1t_sb[:, :, :, c * CH[0]:c * CH[0] + CH[c]].rearrange("p r q j -> p j (r q)"),
                                m_ps[:, 0:CH[c] * P].rearrange("p (j c) -> p j c", c=P)).then_inc(xt_dve, 1)

            def period(u, gg, stat):
                g_no = u * 2 + gg
                turn = gg == 1 and exists(u - 1, PAIRS)
                norm = next_norm(*stat) if stat else None
                for j in range(NJ):
                    n = g_no * NJ + j
                    if exists(g_no - 1, GROUPS) and j == 6:
                        normalize(g_no - 1, 1 - gg)
                    if exists(n, TILES):
                        mask_and_max(n, gg * NJ + j)
                    if exists(g_no + 1, GROUPS) and j == 2 - gg:
                        prep_out(g_no + 1, 1 - gg)
                    if norm and j in (0, 1, 3, 5):
                        next(norm)
                    if turn and j in (1, 3, 4):
                        x1_stats(u - 1, {1: (0,), 3: (1, 2, 3), 4: (4, 5, 6)}[j])
                    if turn and j in (2, 5):
                        x1t_out(u - 1, j // 3)
                    if exists(n - 2, TILES):
                        lo_parts(g_no - int(j < 2), (j - 2) % NJ, norm if j in (4, 6) else None)

            prep_out(0, 0)
            dve.wait_ge(mask_in, 64)
            all_periods(dve, period)
            dve.wait_ge(x1_stat, PAIRS)
            for _ in combine(stats[:, :, :, :, :].rearrange("p b j n (h s) -> p (b j) (n h) s", s=3), DH, B * NJ,
                             mean[:, :], part[:, :], var[:, :], stat_v, STEPS, stat_pe, 2, 1.0,
                             m_ps[:, 0:B * NJ]):
                pass


def feed_forward(nc, up, down, perm, consts, x1t_dram, stat_dram, zt_dram):
    gate = consts["gate"]
    UNITS = H * NC
    WCOLS = 2 * M
    with ExitStack() as es:
        def sb(name, shape, dt=F32):
            return es.enter_context(nc.sbuf_tensor(name, shape, dt))

        def sem(name):
            return es.enter_context(nc.semaphore(name))

        perm_sb = sb("perm_sb", [P, H], I32)
        rows_of = [sb(f"rows_of{i}", [P, 1], I32) for i in range(2)]
        mean_w = sb("mean_w", [P, ROWS])
        rstd_w = sb("rstd_w", [P, ROWS])
        xg = [sb(f"xg{i}", [P, ROWS]) for i in range(2)]
        w_raw = [sb(f"w_raw{i}", [P, WCOLS]) for i in range(2)]
        w_hi = [sb(f"w_hi{i}", [P, WCOLS], F32R) for i in range(2)]
        w_lo = [sb(f"w_lo{i}", [P, WCOLS], F32R) for i in range(2)]
        centered = sb("centered", [P, COLS])
        xnorm = [sb(f"xnorm{i}", [P, COLS]) for i in range(2)]
        x_hi = [sb(f"x_hi{i}", [P, COLS], F32R) for i in range(2)]
        x_lo = [sb(f"x_lo{i}", [P, COLS], F32R) for i in range(2)]
        hid = [sb(f"hid{i}", [P, MC, COLS]) for i in range(2)]
        hid_hi = [sb(f"hid_hi{i}", [P, MC, COLS], F32R) for i in range(2)]
        hid_lo = [sb(f"hid_lo{i}", [P, MC, COLS], F32R) for i in range(2)]
        up_ps = [es.enter_context(nc.psum_tensor(f"up_ps{i}", [P, 2, 512], F32)) for i in range(2)]
        dn_ps = es.enter_context(nc.psum_tensor("dn_ps", [P, 512], F32))

        perm_in = sem("perm_in")
        stats_in = sem("stats_in")
        weights_in = [sem(f"weights_in{i}") for i in range(2)]
        rows_set = sem("rows_set")
        gathered = [sem(f"gathered{i}") for i in range(2)]
        scattered = [sem(f"scattered{i}") for i in range(2)]
        weights_cut = sem("weights_cut")
        x_centered = sem("x_centered")
        x_normed = sem("x_normed")
        x_cut = sem("x_cut")
        up_done = sem("up_done")
        gelu_done = sem("gelu_done")
        hid_hi_done = sem("hid_hi_done")
        hid_lo_done = sem("hid_lo_done")
        down_done = sem("down_done")
        z_done = sem("z_done")
        pool_passed = sem("ff_pool_passed")

        block = es.enter_context(nc.Block())

        def cols(c):
            return bass.ds(c * COLS, COLS)

        def run(eng, unit):
            def pair(hp, first=False):
                for hh in range(2):
                    head = hp * 2 + hh
                    unit(head, hh, 0, first and hh == 0)
                    unit(head, hh, 1, first and hh == 0)
                    with eng.Fori(1, NC // 2) as cc:
                        unit(head, hh, cc * 2, False, even=True)
                        unit(head, hh, cc * 2 + 1, False, even=False)
            pair(0, first=True)
            with eng.Fori(1, H // 2) as hp:
                pair(hp)

        @block.sync
        def _(sp):
            sp.dma_start(perm_sb[:, :], perm.rearrange("(h p) -> p h", p=P), allow_slow_non_contiguous=True).then_inc(perm_in, 16)
            sp.dma_start(mean_w[:, :], stat_dram[0].partition_broadcast(P)).then_inc(stats_in, 16)
            sp.dma_start(rstd_w[:, :], stat_dram[1].partition_broadcast(P)).then_inc(stats_in, 16)

            def load_weights(head, hh):
                sp.dma_start(w_raw[hh][:, 0:M], up[head]).then_inc(weights_in[hh], 16)
                sp.dma_start(w_raw[hh][:, M:WCOLS].rearrange("p (m d) -> p m d", m=MC),
                             down[head].rearrange("(m p) d -> p m d", p=P)).then_inc(weights_in[hh], 16)

            load_weights(0, 0)
            load_weights(1, 1)
            with sp.Fori(1, H // 2) as hp:
                for hh in range(2):
                    sp.wait_ge(weights_cut, hp * 4 - 2 + 2 * hh)
                    load_weights(hp * 2 + hh, hh)

        @block.gpsimd
        def _(pool):
            pool.wait_ge(perm_in, 16)

            def gather(head, hh):
                pool.sem_inc(pool_passed, 1)
                pool.tensor_copy(rows_of[hh][:, :], perm_sb[:, bass.ds(head, 1)]).then_inc(rows_set, 1)
                pool.wait_ge(rows_set, head + 1)
                pool.sem_inc(pool_passed, 1)
                pool.indirect_dma_start(
                    out=xg[hh][:, :], out_offset=None, in_=x1t_dram,
                    in_offset=bass.IndirectOffsetOnAxis(ap=rows_of[hh][:, :].bitcast(U32), axis=0),
                ).then_inc(gathered[hh], 16)

            def scatter(head, hh):
                pool.wait_ge(z_done, (head + 1) * NC)
                pool.sem_inc(pool_passed, 1)
                pool.indirect_dma_start(
                    out=zt_dram, out_offset=bass.IndirectOffsetOnAxis(ap=rows_of[hh][:, :].bitcast(U32), axis=0),
                    in_=xg[hh][:, :], in_offset=None,
                ).then_inc(scattered[hh], 16)

            def cut_weights(head, hh, lag):
                pool.wait_ge(weights_in[hh], ((head >> 1) + 1) * 32)
                if lag:
                    pool.wait_ge(down_done, (head - 1) * NC)
                pool.sem_inc(pool_passed, 1)
                pool.tensor_copy(w_hi[hh][:, :], w_raw[hh][:, :]).then_inc(weights_cut, 1)
                pool.wait_ge(weights_cut, head * 2 + 1)
                pool.sem_inc(pool_passed, 1)
                pool.tensor_tensor(w_lo[hh][:, :], w_raw[hh][:, :], w_hi[hh][:, :].bitcast(F32),
                                   ALU.subtract).then_inc(weights_cut, 1)

            def normalize(head, hh, c, k, par, lag):
                pool.wait_ge(gathered[hh], ((head >> 1) + 1) * 16)
                if lag or c >= 1:
                    pool.wait_ge(x_normed, k)
                pool.sem_inc(pool_passed, 1)
                pool.tensor_tensor(centered[:, :], xg[hh][:, cols(c)], mean_w[:, cols(c)],
                                   ALU.subtract).then_inc(x_centered, 1)
                pool.wait_ge(x_centered, k + 1)
                if lag or c >= 2:
                    pool.wait_ge(x_cut, k * 2 - 2)
                pool.sem_inc(pool_passed, 1)
                pool.tensor_tensor(xnorm[par][:, :], centered[:, :], rstd_w[:, cols(c)],
                                   ALU.mult).then_inc(x_normed, 1)

            pool.wait_ge(stats_in, 32)
            gather(0, 0)
            gather(1, 1)
            cut_weights(0, 0, lag=False)

            def head_units(head, hh, first=False, last=False):
                k = head * NC
                for c in range(3):
                    normalize(head, hh, c, k + c, c % 2, lag=not first)
                if not last:
                    cut_weights(head + 1, 1 - hh, lag=not first)
                if not first:
                    scatter(head - 1, 1 - hh)
                for c in range(3, 6):
                    normalize(head, hh, c, k + c, c % 2, lag=True)
                if not first and not last:
                    pool.wait_ge(scattered[1 - hh], ((head + 1) >> 1) * 16)
                    gather(head + 1, 1 - hh)
                for c in range(6, NC):
                    normalize(head, hh, c, k + c, c % 2, lag=True)

            head_units(0, 0, first=True)
            head_units(1, 1)
            with pool.Fori(1, H // 2 - 1) as hp:
                head_units(hp * 2, 0)
                head_units(hp * 2 + 1, 1)
            head_units(H - 2, 0)
            head_units(H - 1, 1, last=True)
            scatter(H - 1, 1)
            pool.wait_ge(scattered[0], 16 * (H // 2))
            pool.wait_ge(scattered[1], 16 * (H // 2))

        @block.tensor
        def _(pe):
            def go_up(hh, k, par, new_head, lag):
                if new_head:
                    pe.wait_ge(weights_cut, (k >> 3) * 2 + 2)
                pe.wait_ge(x_cut, k * 2 + 2)
                for half in range(2):
                    if lag:
                        pe.wait_ge(gelu_done, k * 2 - 1 + half)
                    for i in range(2):
                        m = half * 2 + i
                        dst = up_ps[half][:, i, 0:COLS]
                        pe.matmul(dst, w_hi[hh][:, m * P:(m + 1) * P], x_hi[par][:, :], start=True, stop=False)
                        pe.matmul(dst, w_hi[hh][:, m * P:(m + 1) * P], x_lo[par][:, :], start=False, stop=False)
                        last = pe.matmul(dst, w_lo[hh][:, m * P:(m + 1) * P], x_hi[par][:, :], start=False, stop=True)
                    last.then_inc(up_done, 1)

            def go_down(hh, k, par, lag):
                pe.wait_ge(hid_lo_done, k * 2 + 2)
                if lag:
                    pe.wait_ge(z_done, k)
                for m in range(MC):
                    w = slice(M + m * P, M + (m + 1) * P)
                    pe.matmul(dn_ps[:, 0:COLS], w_hi[hh][:, w], hid_hi[par][:, m, :], start=(m == 0), stop=False)
                    pe.matmul(dn_ps[:, 0:COLS], w_hi[hh][:, w], hid_lo[par][:, m, :], start=False, stop=False)
                    last = pe.matmul(dn_ps[:, 0:COLS], w_lo[hh][:, w], hid_hi[par][:, m, :], start=False,
                                     stop=(m == MC - 1))
                last.then_inc(down_done, 1)

            def unit(head, hh, c, first, even=None):
                k = head * NC + c
                par = c % 2 if even is None else int(not even)
                go_up(hh, k, par, even is None and c == 0, lag=not (first and c == 0))
                if not (first and c == 0):
                    go_down(1 - hh if even is None and c == 0 else hh, k - 1, 1 - par, lag=not (first and c == 1))

            run(pe, unit)
            go_down(1, UNITS - 1, 1, lag=True)

        @block.scalar
        def _(act):
            def unit(head, hh, c, first, even=None):
                k = head * NC + c
                par = c % 2 if even is None else int(not even)
                for half in range(2):
                    at = slice(half * 2, half * 2 + 2)
                    act.wait_ge(up_done, k * 2 + half + 1)
                    if not first:
                        act.wait_ge(hid_lo_done, k * 2 - 3 + half)
                    act.activation(hid[par][:, at, :], up_ps[half][:, :, 0:COLS], ACT.Gelu).then_inc(gelu_done, 1)
                for half in range(2):
                    at = slice(half * 2, half * 2 + 2)
                    act.wait_ge(gelu_done, k * 2 + half + 1)
                    if not first:
                        act.wait_ge(down_done, k - 1)
                    act.activation(hid_hi[par][:, at, :], hid[par][:, at, :], ACT.Copy).then_inc(hid_hi_done, 1)

            run(act, unit)

        @block.vector
        def _(dve):
            def cut_x(k, par, first):
                dve.wait_ge(x_normed, k + 1)
                if not first:
                    dve.wait_ge(up_done, k * 2 - 2)
                dve.tensor_copy(x_hi[par][:, :], xnorm[par][:, :]).then_inc(x_cut, 1)
                dve.wait_ge(x_cut, k * 2 + 1)
                dve.tensor_tensor(x_lo[par][:, :], xnorm[par][:, :], x_hi[par][:, :].bitcast(F32),
                                  ALU.subtract).then_inc(x_cut, 1)

            def cut_hidden(k, par):
                for half in range(2):
                    at = slice(half * 2, half * 2 + 2)
                    dve.wait_ge(hid_hi_done, k * 2 + half + 1)
                    dve.tensor_tensor(hid_lo[par][:, at, :], hid[par][:, at, :], hid_hi[par][:, at, :].bitcast(F32),
                                      ALU.subtract).then_inc(hid_lo_done, 1)

            def result(hh, c, k):
                dve.wait_ge(down_done, k + 1)
                dve.scalar_tensor_tensor(out=xg[hh][:, cols(c)], in0=dn_ps[:, 0:COLS], scalar=gate[:, 1:2],
                                         in1=xg[hh][:, cols(c)], op0=ALU.mult, op1=ALU.add).then_inc(z_done, 1)

            def unit(head, hh, c, first, even=None):
                k = head * NC + c
                par = c % 2 if even is None else int(not even)
                cut_x(k, par, first)
                if not (first and c == 0):
                    cut_hidden(k - 1, 1 - par)
                if not first:
                    back = even is None
                    result(1 - hh if back else hh, c + NC - 2 if back else c - 2, k - 2)

            run(dve, unit)
            cut_hidden(UNITS - 1, 1)
            result(1, NC - 2, UNITS - 2)
            result(1, NC - 1, UNITS - 1)


def transpose_back(nc, consts, zt_dram, out):
    ident = consts["ident"]
    RING = 4
    TILES = ROWS // P
    F = D // P
    zt_view = zt_dram.rearrange("(f p) c -> p f c", p=P)
    out_view = out.rearrange("b q d -> (b q) d")
    with ExitStack() as es:
        z_in = [es.enter_context(nc.sbuf_tensor(f"z_in{i}", [P, F, P], F32)) for i in range(RING)]
        z_out = [es.enter_context(nc.sbuf_tensor(f"z_out{i}", [P, D], F32)) for i in range(RING)]
        z_ps = [es.enter_context(nc.psum_tensor(f"z_ps{i}", [P, D], F32)) for i in range(2)]
        loaded = [es.enter_context(nc.semaphore(f"loaded{i}")) for i in range(RING)]
        stored = [es.enter_context(nc.semaphore(f"stored{i}")) for i in range(RING)]
        turned = es.enter_context(nc.semaphore("z_turned"))
        act_out = es.enter_context(nc.semaphore("z_act_out"))
        dve_out = es.enter_context(nc.semaphore("z_dve_out"))
        block = es.enter_context(nc.Block())

        def ring(eng, tile):
            for s in range(RING):
                tile(s, s, 0, True)
            with eng.Fori(1, TILES // RING) as i:
                for s in range(RING):
                    tile(i * RING + s, s, i, False)

        @block.sync
        def _(sp):
            def tile(i, s, turn, first):
                if not first:
                    sp.wait_ge(turned, i - RING + 1)
                sp.dma_start(z_in[s][:, :, :], zt_view[:, :, bass.ds(i * P, P)]).then_inc(loaded[s], 16)

            ring(sp, tile)

        @block.tensor
        def _(pe):
            def tile(i, s, turn, first):
                pe.wait_ge(loaded[s], turn * 16 + 16)
                if not first or s >= 2:
                    pe.wait_ge(act_out, i - 1)
                    pe.wait_ge(dve_out, i - 1)
                for f in range(F):
                    last = pe.transpose(z_ps[s % 2][:, f * P:(f + 1) * P], z_in[s][:, f, :], ident[:, :])
                last.then_inc(turned, 1)

            ring(pe, tile)

        @block.scalar
        def _(act):
            def tile(i, s, turn, first):
                act.wait_ge(turned, i + 1)
                if not first:
                    act.wait_ge(stored[s], turn * 16)
                act.activation(z_out[s][:, 0:D // 2], z_ps[s % 2][:, 0:D // 2], ACT.Copy).then_inc(act_out, 1)
                act.wait_ge(act_out, i + 1)
                act.wait_ge(dve_out, i + 1)
                act.dma_start(out_view[bass.ds(i * P, P)], z_out[s][:, :]).then_inc(stored[s], 16)

            ring(act, tile)
            for s in range(RING):
                act.wait_ge(stored[s], TILES // RING * 16)

        @block.vector
        def _(dve):
            def tile(i, s, turn, first):
                dve.wait_ge(turned, i + 1)
                if not first:
                    dve.wait_ge(stored[s], turn * 16)
                dve.tensor_copy(z_out[s][:, D // 2:D], z_ps[s % 2][:, D // 2:D]).then_inc(dve_out, 1)

            ring(dve, tile)


_INS = ["x", "ctx_1024", "mask_SxS2_ff0", "g_xattn", "g_ffn", "L0_ffn_up", "L0_ffn_down", "L0_ffn_perm"]
_OUTS = [((B, SQ, D), "float32")]


def kernel(**inputs):
    import numpy as _np
    import concourse.bacc as _bacc
    from concourse import mybir as _mybir
    from concourse.bass_utils import run_bass_kernel_spmd as _run

    nc = _bacc.Bacc("TRN2", target_bir_lowering=False, num_devices=1)
    arrays, args = {}, []
    for name in _INS:
        a = _np.ascontiguousarray(inputs[name])
        arrays[f"in_{name}_dram"] = a
        args.append(nc.dram_tensor(f"in_{name}_dram", a.shape, _mybir.dt.from_np(a.dtype), kind="ExternalInput").ap())
    for i, (shape, dtype) in enumerate(_OUTS):
        dt = _mybir.dt.from_np(_np.dtype(dtype))
        args.append(nc.dram_tensor(f"out_{i}_dram", shape, dt, kind="ExternalOutput").ap())
    build(nc, *args)
    r = _run(nc, [arrays], core_ids=[0])
    return r.results[0]["out_0_dram"]
```

```python
from contextlib import ExitStack

import concourse.bass as bass
from concourse import mybir

F32 = mybir.dt.float32
F32R = mybir.dt.float32r
I32 = mybir.dt.int32
U32 = mybir.dt.uint32
ALU = mybir.AluOpType
ACT = mybir.ActivationFunctionType
AX_X = mybir.AxisListType.X

P = 128
B, SQ, D = 16, 224, 2048
T, C = 750, 512
NG, NR, DH = 8, 4, 64
ROWS = B * SQ
PJ = P // NR
NJ = SQ // PJ
NT, TT = 6, T // 6
NPAIR = NG // 2
PAIRS = B * NPAIR
CH = (4, 3)
QW = NJ * P
EPS = 1e-5
STEPS = 7
HALF = NT // 2
KC = 4
GROUPS = B * NG
TILES = GROUPS * NJ
PER_BATCH = NPAIR - 1
JS, JSTEP = 3, 2
NSTEPS = 8
H, M = 16, 512
MC = M // P
COLS, NC = 448, 8
SCALE = float(DH)


def await_(eng, semaphore, count):
    if not isinstance(count, int) or count > 0:
        eng.wait_ge(semaphore, count)


def exists(number, end):
    return not isinstance(number, int) or 0 <= number < end


def build(nc, x, ctx_in, mask, g_x, g_f, up, down, perm, out):
    x1t_dram = nc.dram_tensor("x1t_scratch", [D, ROWS], F32).ap()
    zt_dram = nc.dram_tensor("zt_scratch", [D, ROWS], F32).ap()
    stat_dram = nc.dram_tensor("stat_scratch", [2, ROWS], F32).ap()

    with ExitStack() as keep:
        consts = {
            "ident": keep.enter_context(nc.sbuf_tensor("ident", [P, P], F32)),
            "gate": keep.enter_context(nc.sbuf_tensor("gate", [P, 2], F32)),
            "ones": keep.enter_context(nc.sbuf_tensor("ones", [P, 1], F32)),
            "mean": keep.enter_context(nc.sbuf_tensor("mean", [P, B * NJ], F32)),
            "rstd": keep.enter_context(nc.sbuf_tensor("rstd", [P, B * NJ], F32)),
            "var": keep.enter_context(nc.sbuf_tensor("var", [P, B * NJ], F32)),
            "power": keep.enter_context(nc.sbuf_tensor("power", [P, B * NJ], F32)),
        }
        attention(nc, x, ctx_in, mask, g_x, g_f, consts, x1t_dram)
        feed_forward(nc, up, down, perm, consts, x1t_dram, stat_dram, zt_dram)
        transpose_back(nc, consts, zt_dram, out)


def attention(nc, x, ctx_in, mask, g_x, g_f, consts, x1t_dram):
    ident, gate, ones = consts["ident"], consts["gate"], consts["ones"]
    mean, rstd, var, power = (consts[name] for name in ("mean", "rstd", "var", "power"))
    x_view = x.rearrange("b (p j) (g r d) -> b r p j g d", j=NJ, g=NG, r=NR)
    ctx_view = ctx_in.rearrange("b (t p) c -> b p t c", p=TT)
    mask_view = mask.rearrange("(p j) t -> p j t", j=NJ)
    x1t_view = x1t_dram.rearrange("(n gg r d) c -> n gg d r c", n=NPAIR, gg=2, r=NR)

    with ExitStack() as es:
        def sb(name, shape, dt=F32):
            return es.enter_context(nc.sbuf_tensor(name, shape, dt))

        def ps(name, cols):
            return es.enter_context(nc.psum_tensor(name, [P, cols], F32))

        def sem(name):
            return es.enter_context(nc.semaphore(name))

        mask_sb = sb("mask_sb", [P, NJ, T])
        x_raw = sb("x_raw", [P, 2, NJ, NG, DH])
        ctx_sb = sb("ctx_sb", [TT, 2, NT, C])
        k_split = [sb(f"k_split{i}", [TT, NT, 2, DH], F32R) for i in range(2)]
        values = [sb(f"values{i}", [TT, NT, 2 * DH], F32R) for i in range(2)]
        q_split = sb("q_split", [P, NJ, 2 * DH], F32R)
        qt = [sb(f"qt{i}", [P, QW], F32R) for i in range(2)]
        kt = [sb(f"kt{i}", [P, 2, T], F32R) for i in range(2)]
        neg_scores = [sb(f"neg_scores{i}", [P, T]) for i in range(2)]
        probs = [sb(f"probs{i}", [P, T]) for i in range(2)]
        pt_hi = [sb(f"pt_hi{c}", [TT, CH[c], NT, P], F32R) for c in range(2)]
        pt_lo = [sb(f"pt_lo{c}", [TT, CH[c], NT, P], F32R) for c in range(2)]
        att_t = sb("att_t", [P, QW])
        att_n = [sb(f"att_n{i}", [P, NJ, DH]) for i in range(2)]
        x1_pair = sb("x1_pair", [P, NJ, 2, DH])
        x1t_sb = sb("x1t_sb", [P, NR, PJ, NJ])
        ident_r = sb("ident_r", [P, P], F32R)
        xn = sb("xn", [P, NJ, DH])
        neg_max = sb("neg_max", [P, 2 * NJ])
        row_sum = sb("row_sum", [P, 2, NJ])
        row_inv = sb("row_inv", [P, NJ])
        stats = sb("stats", [P, B, NJ, NPAIR, 6])
        part = sb("part", [P, B * NJ])
        next_triples = sb("next_triples", [P, JS, 2, 3])
        next_part = sb("next_part", [P, JS])
        next_var = sb("next_var", [P, JS])
        same = sb("same", [P, P])
        fold = sb("fold", [P, DH])

        s_ps = [ps(f"s_ps{i}", 1024) for i in range(2)]
        pt_ps = [ps(f"pt_ps{i}", 512) for i in range(2)]
        sums_ps = pt_ps[1][:, HALF * P:HALF * P + JS]
        o_ps = ps("o_ps", 512)
        m_ps = ps("m_ps", 512)

        gates_in = sem("gates_in")
        mask_in = sem("mask_in")
        zeroed = sem("zeroed")
        marked = sem("marked")
        gated = sem("gated")
        folded = sem("folded")
        powered = sem("powered")
        stat_v = sem("stat_v")
        stat_taken = sem("stat_taken")
        stat_pe = sem("stat_pe")
        stat_done = sem("stat_done")
        next_stat = sem("next_stat")
        next_sum = sem("next_sum")
        next_rstd = sem("next_rstd")
        x_arrived = sem("x_arrived")
        ctx_arrived = sem("ctx_arrived")
        k_cut = sem("k_cut")
        q_cut = sem("q_cut")
        v_put = sem("v_put")
        prep_filled = sem("prep_filled")
        prep_act = sem("prep_act")
        swapped = sem("swapped")
        scored = sem("scored")
        masked = sem("masked")
        expd = sem("expd")
        turned = [sem(f"turned{i}") for i in range(2)]
        hi_out = [sem(f"hi_out{i}") for i in range(2)]
        lo_out = [sem(f"lo_out{i}") for i in range(2)]
        weighed = sem("weighed")
        att_out = sem("att_out")
        summed = sem("summed")
        inverted = sem("inverted")
        normed = sem("normed")
        added = sem("added")
        x1_stat = sem("x1_stat")
        xt_filled = sem("xt_filled")
        xt_act = sem("xt_act")
        xt_dve = sem("xt_dve")
        x1_stored = sem("x1_stored")
        dve_passed = sem("dve_passed")
        pool_passed = sem("pool_passed")
        sp_passed = sem("sp_passed")

        block = es.enter_context(nc.Block())

        def load_x(sp, b, par, s):
            for r in range(NR):
                sp.dma_start(x_raw[PJ * r:PJ * (r + 1), par], x_view[b, r]).then_inc(s, 16)

        def load_ctx(sp, b, par):
            sp.dma_start(ctx_sb[:, par], ctx_view[b]).then_inc(ctx_arrived, 16)

        @block.sync
        def _(sp):
            sp.dma_start(gate[:, 0:1], g_x.partition_broadcast(P)).then_inc(gates_in, 16)
            sp.dma_start(gate[:, 1:2], g_f.partition_broadcast(P)).then_inc(gates_in, 16)
            load_x(sp, 0, 0, x_arrived)
            load_ctx(sp, 0, 0)
            for r in range(NR):
                sp.dma_start(mask_sb[PJ * r:PJ * (r + 1)], mask_view).then_inc(mask_in, 16)
            sp.wait_ge(ctx_arrived, 16)
            load_ctx(sp, 1, 1)
            sp.wait_ge(x_arrived, 64)
            load_x(sp, 1, 1, x_arrived)

            def store_pair(b, n):
                u = b * NPAIR + n
                sp.wait_ge(xt_act, u + 1)
                sp.sem_inc(sp_passed, 1)
                sp.wait_ge(xt_dve, u + 1)
                sp.sem_inc(sp_passed, 1)
                for gg in range(2):
                    sp.dma_start(x1t_view[n, gg][:, :, bass.ds(b * SQ, SQ)],
                                 x1t_sb[DH * gg:DH * (gg + 1)].rearrange("p r q j -> p r (q j)")
                                 ).then_inc(x1_stored, 16)

            def swap_keys(g_no, slot):
                sp.wait_ge(prep_act, g_no * 4 + 2)
                for half in range(2):
                    sp.dma_start(kt[slot][DH * half:DH * (half + 1), 1, :].bitcast(F32),
                                 kt[slot][DH * (1 - half):DH * (2 - half), 0, :].bitcast(F32)).then_inc(swapped, 16)

            def pair(u, load=None):
                if exists(u * 2 + 1, GROUPS):
                    swap_keys(u * 2 + 1, 1)
                if load:
                    b, par = load
                    sp.wait_ge(ctx_arrived, b * 16)
                    sp.sem_inc(sp_passed, 1)
                    sp.wait_ge(k_cut, (b - 1) * (2 * NG))
                    sp.sem_inc(sp_passed, 1)
                    load_ctx(sp, b, par)
                    sp.wait_ge(x_arrived, b * 64)
                    sp.sem_inc(sp_passed, 1)
                    sp.wait_ge(added, (b - 1) * NG)
                    sp.sem_inc(sp_passed, 1)
                    load_x(sp, b, par, x_arrived)
                if exists(u * 2 + 2, GROUPS):
                    swap_keys(u * 2 + 2, 0)
                if exists(u - 1, PAIRS):
                    store_pair(((u - 1) >> 2) & (B - 1), (u - 1) & (NPAIR - 1))

            swap_keys(0, 0)
            pair(0)
            with sp.Fori(1, NPAIR) as u:
                pair(u)
            with sp.Fori(0, B // 2 - 1) as i:
                for par in range(2):
                    b = i * 2 + par + 1
                    pair(b * NPAIR, (b + 1, par))
                    with sp.Fori(1, NPAIR) as n:
                        pair(b * NPAIR + n)
            with sp.Fori(PAIRS - NPAIR, PAIRS - 1) as u:
                pair(u)
            pair(PAIRS - 1)
            pair(PAIRS)
            sp.wait_ge(x1_stored, 32 * PAIRS)

        def ctx_group(g_no):
            return ctx_sb[:, (g_no >> 3) & 1, :, bass.ds((g_no & 7) * DH, DH)]

        def x_group(g_no):
            return x_raw[:, (g_no >> 3) & 1, :, g_no & 7, :]

        def of_batch(t, g_no):
            return t[:, bass.ds(((g_no >> 3) & (B - 1)) * NJ, NJ)].unsqueeze(2).to_broadcast([P, NJ, DH])

        def all_periods(eng, period):
            def pair(u, stat=None):
                for gg in range(2):
                    period(u, gg, stat if gg == 0 else None)
            pair(0)
            pair(1, (1, 0, 0))
            with eng.Fori(2, NPAIR) as n:
                pair(n, (1, n - 1, n - 1))
            with eng.Fori(1, B - 1) as b:
                pair(b * NPAIR)
                with eng.Fori(1, NPAIR) as n:
                    pair(b * NPAIR + n, (b + 1, n - 1, b * PER_BATCH + n - 1))
            with eng.Fori(PAIRS - NPAIR, PAIRS - 1) as u:
                pair(u)
            pair(PAIRS - 1)
            pair(PAIRS)

        @block.gpsimd
        def _(pool):
            pool.memset(ident[:, :], 0.0).then_inc(zeroed, 1)
            pool.memset(same[:, :], 0.0).then_inc(zeroed, 1)
            pool.memset(power[:, :], -0.5).then_inc(powered, 1)
            pool.memset(ones[:, :], 1.0).then_inc(powered, 1)
            pool.wait_ge(zeroed, 2)
            pool.affine_select(out=ident[:, :], in_=ident[:, :], compare_op=ALU.not_equal, fill=1.0,
                               base=0, pattern=[[-1, P]], channel_multiplier=1).then_inc(marked, 1)
            for k in range(2 * NR - 1):
                pool.wait_ge(marked, k + 1)
                pool.affine_select(out=same[:, :], in_=same[:, :], compare_op=ALU.not_equal, fill=1.0,
                                   base=PJ * (k - NR + 1), pattern=[[-1, P]],
                                   channel_multiplier=1).then_inc(marked, 1)
            pool.tensor_copy(ident_r[:, :], ident[:, :]).then_inc(marked, 1)
            pool.wait_ge(powered, 2)


            def next_deviation(b, m, k):
                pool.wait_ge(next_stat, k * NSTEPS + NSTEPS)
                pool.sem_inc(pool_passed, 1)
                pool.tensor_tensor(rstd[:, bass.ds(b * NJ + m, JS, JSTEP)], next_var[:, :],
                                   power[:, 0:JS], ALU.pow).then_inc(next_rstd, 1)

            def cut_context(g_no, slot):
                pool.wait_ge(ctx_arrived, ((g_no >> 3) + 1) * 16)
                await_(pool, prep_filled, g_no * 4 - 6)
                await_(pool, v_put, g_no - 1)
                pool.sem_inc(pool_passed, 1)
                pool.tensor_tensor(k_split[slot][:, :, 0, :], ctx_group(g_no),
                                   ones[0:TT, :].unsqueeze(2).to_broadcast([TT, NT, DH]),
                                   ALU.mult).then_inc(k_cut, 1)
                pool.wait_ge(k_cut, g_no * 2 + 1)
                pool.sem_inc(pool_passed, 1)
                pool.tensor_tensor(k_split[slot][:, :, 1, :], ctx_group(g_no), k_split[slot][:, :, 0, :].bitcast(F32),
                                   ALU.subtract).then_inc(k_cut, 1)

            def cut_queries(g_no):
                pool.wait_ge(x_arrived, ((g_no >> 3) + 1) * 64)
                await_(pool, next_rstd, (g_no >> 3) * PER_BATCH)
                await_(pool, prep_filled, g_no * 4)
                await_(pool, q_cut, g_no * 4)
                pool.sem_inc(pool_passed, 1)
                pool.tensor_tensor(xn[:, :, :], x_group(g_no), of_batch(mean, g_no), ALU.subtract).then_inc(q_cut, 1)
                pool.wait_ge(q_cut, g_no * 4 + 1)
                pool.sem_inc(pool_passed, 1)
                pool.tensor_tensor(xn[:, :, :], xn[:, :, :], of_batch(rstd, g_no), ALU.mult).then_inc(q_cut, 1)
                pool.wait_ge(q_cut, g_no * 4 + 2)
                pool.sem_inc(pool_passed, 1)
                pool.tensor_tensor(q_split[:, :, 0:DH], xn[:, :, :],
                                   ones[:, :].unsqueeze(2).to_broadcast([P, NJ, DH]), ALU.mult).then_inc(q_cut, 1)
                pool.wait_ge(q_cut, g_no * 4 + 3)
                pool.sem_inc(pool_passed, 1)
                pool.tensor_tensor(q_split[:, :, DH:2 * DH], xn[:, :, :], q_split[:, :, 0:DH].bitcast(F32),
                                   ALU.subtract).then_inc(q_cut, 1)

            def put_values(g_no, slot):
                pool.wait_ge(k_cut, g_no * 2 + 2)
                await_(pool, weighed, g_no * 2 - 2)
                pool.sem_inc(pool_passed, 1)
                src = k_split[slot][:, :, :, :].rearrange("p t s d -> p t (s d)").bitcast(F32)
                pool.tensor_tensor(values[slot][:, :, :], src,
                                   ones[0:TT, :].unsqueeze(2).to_broadcast([TT, NT, 2 * DH]),
                                   ALU.mult).then_inc(v_put, 1)

            def add_x(g_no, gg):
                pool.wait_ge(normed, g_no + 1)
                if gg == 0:
                    await_(pool, xt_filled, g_no)
                    await_(pool, x1_stat, g_no >> 1)
                pool.sem_inc(pool_passed, 1)
                pool.tensor_tensor(x1_pair[:, :, gg, :], att_n[gg][:, :, :], x_group(g_no),
                                   ALU.add).then_inc(added, 1)

            def period(u, gg, stat):
                g_no = u * 2 + gg
                if exists(g_no + 1, GROUPS):
                    cut_queries(g_no + 1)
                if exists(g_no + 2, GROUPS):
                    cut_context(g_no + 2, gg)
                if exists(g_no + 1, GROUPS):
                    put_values(g_no + 1, 1 - gg)
                if exists(g_no - 1, GROUPS):
                    add_x(g_no - 1, 1 - gg)
                if stat:
                    next_deviation(*stat)

            pool.wait_ge(stat_v, STEPS)
            pool.tensor_tensor(rstd[:, 0:NJ], var[:, 0:NJ], power[:, 0:NJ], ALU.pow).then_inc(stat_done, 1)
            pool.wait_ge(stat_done, 1)
            cut_queries(0)
            cut_context(0, 0)
            cut_context(1, 1)
            put_values(0, 0)
            all_periods(pool, period)

        @block.tensor
        def _(pe):
            def sum_partitions(k, n):
                for step in range(2):
                    pe.wait_ge(stat_v, STEPS * k + (1, 6)[step])
                    if k == 0 and step == 0:
                        pe.wait_ge(marked, 2 * NR + 1)
                    if k == 1 and step == 0:
                        pe.wait_ge(xt_dve, PAIRS)
                    pe.matmul(m_ps[:, 0:n], same[:, :], part[:, 0:n], start=True, stop=True).then_inc(stat_pe, 1)

            def sum_next(k, step):
                pe.wait_ge(next_stat, k * NSTEPS + (2, 7)[step])
                pe.matmul(sums_ps, same[:, :], next_part[:, :], start=True, stop=True).then_inc(next_sum, 1)

            def prep(g_no, slot, piece, free, count):
                if piece == 0:
                    pe.wait_ge(k_cut, g_no * 2 + 2)
                if piece == 2:
                    pe.wait_ge(q_cut, g_no * 4 + 4)
                await_(pe, free, count)
                if piece < 2:
                    for i in range((KC, NT - KC)[piece]):
                        last = pe.matmul(m_ps[:, i * (TT + 1):(i + 1) * (TT + 1)],
                                         k_split[slot][:, piece * KC + i, :, :].rearrange("p s d -> p (s d)"),
                                         ident_r[0:TT, 0:TT + 1], start=True, stop=True)
                else:
                    j0 = (0, CH[0])[piece - 2]
                    for j in range(CH[piece - 2]):
                        last = pe.matmul(m_ps[:, j * P:(j + 1) * P], q_split[:, j0 + j, :], ident_r[:, :],
                                         start=True, stop=True)
                last.then_inc(prep_filled, 1)

            def scores(g_no, slot, j):
                n = g_no * NJ + j
                buf = (slot * NJ + j) % 2
                if j == 0:
                    pe.wait_ge(prep_act, g_no * 4 + 3)
                    pe.wait_ge(swapped, g_no * 32 + 32)
                if j == CH[0]:
                    pe.wait_ge(prep_act, g_no * 4 + 4)
                await_(pe, masked, n - 1)
                q = qt[slot][:, j * P:(j + 1) * P]
                for c0, c1 in ((0, 512), (512, T)):
                    pe.matmul(s_ps[buf][:, c0:c1], q, kt[slot][:, 0, c0:c1], start=True, stop=False)
                    last = pe.matmul(s_ps[buf][:, c0:c1], q, kt[slot][:, 1, c0:c1], start=False, stop=True)
                last.then_inc(scored, 1)

            def turn_probs(n, buf, sums=None):
                pe.wait_ge(expd, n + 1)
                for half in range(2):
                    await_(pe, lo_out[half], n)
                    if sums and half == 1:
                        sum_next(*sums)
                    for k in range(HALF):
                        t = half * HALF + k
                        last = pe.transpose(pt_ps[half][0:TT, k * P:(k + 1) * P],
                                            probs[buf][:, t * TT:(t + 1) * TT], ident[:, :])
                    last.then_inc(turned[half], 1)

            def weigh(g_no, slot, c, third):
                width = CH[c] * P
                if third == 0:
                    pe.wait_ge(lo_out[1], g_no * NJ + (CH[0], NJ)[c])
                    if c == 0:
                        pe.wait_ge(v_put, g_no + 1)
                        await_(pe, normed, g_no)
                    else:
                        pe.wait_ge(att_out, g_no * 2 + 1)
                for t in (2 * third, 2 * third + 1):
                    for k, src in enumerate((pt_hi[c], pt_lo[c])):
                        last = pe.matmul(o_ps[:, 0:width], values[slot][:, t, :], src[:, :, t, :],
                                         start=(t == 0 and k == 0), stop=(t == NT - 1 and k == 1))
                if third == 2:
                    last.then_inc(weighed, 1)

            def fold_parts(g_no):
                pe.wait_ge(att_out, g_no * 2 + 2)
                pe.wait_ge(folded, 2)
                for j in range(NJ):
                    last = pe.matmul(o_ps[:, j * DH:(j + 1) * DH], att_t[:, j * P:(j + 1) * P], fold[:, :],
                                     start=True, stop=True)
                last.then_inc(summed, 1)

            def turn_x1(u, piece):
                if piece == 0:
                    pe.wait_ge(added, u * 2 + 2)
                for j in range(CH[piece]):
                    last = pe.transpose(m_ps[:, j * P:(j + 1) * P],
                                        x1_pair[:, (0, CH[0])[piece] + j, :, :].rearrange("p g d -> p (g d)"),
                                        ident[:, :])
                last.then_inc(xt_filled, 1)

            def period(u, gg, stat):
                g_no = u * 2 + gg
                nxt = exists(g_no + 1, GROUPS)
                nx = g_no + 1
                turn = gg == 1 and exists(u - 1, PAIRS)
                before = exists(g_no - 1, GROUPS)
                for j in range(NJ):
                    n = g_no * NJ + j
                    if exists(n, TILES):
                        scores(g_no, gg, j)
                    if nxt and j == 1 - gg:
                        prep(nx, 1 - gg, 0, prep_act, nx * 4)
                    if nxt and j == 2 - gg:
                        prep(nx, 1 - gg, 1, prep_act, nx * 4 + 1)
                    if turn and j == 3:
                        if nxt:
                            pe.wait_ge(prep_act, nx * 4 + 2)
                        else:
                            pe.wait_ge(prep_act, GROUPS * 4)
                            pe.wait_ge(xt_dve, u - 1)
                        turn_x1(u - 1, 0)
                    if nxt and j == 4:
                        if turn:
                            prep(nx, 1 - gg, 2, xt_act, u)
                        else:
                            prep(nx, 1 - gg, 2, prep_act, nx * 4 + 2)
                    if turn and j == 5:
                        if nxt:
                            pe.wait_ge(prep_act, nx * 4 + 3)
                        else:
                            pe.wait_ge(xt_act, u)
                        turn_x1(u - 1, 1)
                    if nxt and j == 5 + gg:
                        if turn:
                            prep(nx, 1 - gg, 3, xt_dve, u)
                        else:
                            prep(nx, 1 - gg, 3, prep_act, nx * 4 + 3)
                    if exists(n - 2, TILES):
                        turn_probs(n - 2, (gg * NJ + j) % 2,
                                   (stat[2], j // 2 - 2) if stat and j in (4, 6) else None)
                    if before and j < 2:
                        weigh(g_no - 1, 1 - gg, 0, j + 1)
                    if before and j in (2, 3, 4):
                        weigh(g_no - 1, 1 - gg, 1, j - 2)
                    if before and j == 5:
                        fold_parts(g_no - 1)
                    if exists(g_no, GROUPS) and j == 6:
                        weigh(g_no, gg, 0, 0)

            sum_partitions(0, NJ)
            pe.wait_ge(stat_v, STEPS)
            for piece in range(4):
                prep(0, 0, piece, prep_act, piece)
            all_periods(pe, period)
            sum_partitions(1, B * NJ)

        @block.scalar
        def _(act):
            act.wait_ge(gates_in, 32)
            act.activation(gate[:, :], gate[:, :], ACT.Tanh).then_inc(gated, 1)

            def prep_out(g_no, slot, piece):
                act.wait_ge(prep_filled, g_no * 4 + piece + 1)
                if piece == 0:
                    last = act.activation(kt[slot][:, 0, 0:KC * TT].rearrange("p (t c) -> p t c", c=TT),
                                          m_ps[:, 0:KC * (TT + 1)].rearrange("p (t c) -> p t c", c=TT + 1)[:, :, 0:TT],
                                          ACT.Copy)
                elif piece == 1:
                    last = act.activation(kt[slot][:, 0, KC * TT:T].rearrange("p (t c) -> p t c", c=TT),
                                          m_ps[:, 0:(NT - KC) * (TT + 1)].rearrange(
                                              "p (t c) -> p t c", c=TT + 1)[:, :, 0:TT], ACT.Copy)
                elif piece == 2:
                    last = act.activation(qt[slot][:, 0:CH[0] * P], m_ps[:, 0:CH[0] * P], ACT.Copy)
                else:
                    last = act.activation(qt[slot][:, CH[0] * P:QW], m_ps[:, 0:CH[1] * P], ACT.Copy)
                last.then_inc(prep_act, 1)

            def exponentials(n, s):
                act.wait_ge(masked, n + 1)
                await_(act, turned[1], n - 1)
                act.activation(probs[s % 2][:, :], neg_scores[s % 2][:, :], ACT.Exp, bias=neg_max[:, s:s + 1],
                               scale=-1.0, accum_out=row_sum[:, s // NJ, s % NJ:s % NJ + 1]).then_inc(expd, 1)

            def hi_parts(g_no, j):
                n = g_no * NJ + j
                c = int(j >= CH[0])
                if j in (0, CH[0]):
                    await_(act, weighed, g_no * 2 - 1 + c)
                for half in range(2):
                    act.wait_ge(turned[half], n + 1)
                    act.activation(pt_hi[c][:, j - c * CH[0], half * HALF:(half + 1) * HALF, :],
                                   pt_ps[half][0:TT, 0:HALF * P], ACT.Copy).then_inc(hi_out[half], 1)

            def x1t_out(u):
                act.wait_ge(xt_filled, u * 2 + 1)
                await_(act, x1_stored, u * 32)
                act.activation(x1t_sb[:, :, :, 0:CH[0]].rearrange("p r q j -> p j (r q)"),
                               m_ps[:, 0:CH[0] * P].rearrange("p (j c) -> p j c", c=P),
                               ACT.Copy).then_inc(xt_act, 1)

            def att_evacuate(g_no, c):
                act.wait_ge(weighed, g_no * 2 + c + 1)
                if c == 0:
                    await_(act, summed, g_no)
                act.activation(att_t[:, c * CH[0] * P:(c * CH[0] + CH[c]) * P], o_ps[:, 0:CH[c] * P],
                               ACT.Copy).then_inc(att_out, 1)

            def period(u, gg, stat):
                g_no = u * 2 + gg
                for j in range(NJ):
                    n = g_no * NJ + j
                    if exists(n - 1, TILES):
                        exponentials(n - 1, (gg * NJ + j - 1) % (2 * NJ))
                    if exists(g_no - 1, GROUPS) and j in (2, 5):
                        att_evacuate(g_no - 1, j // 3)
                    if exists(g_no + 1, GROUPS) and j in (1 - gg, 2 - gg, 4, 5 + gg):
                        prep_out(g_no + 1, 1 - gg, {1 - gg: 0, 2 - gg: 1, 4: 2, 5 + gg: 3}[j])
                    if gg == 1 and exists(u - 1, PAIRS) and j == 3:
                        x1t_out(u - 1)
                    if exists(n - 2, TILES):
                        hi_parts(g_no - int(j < 2), (j - 2) % NJ)

            for piece in range(4):
                prep_out(0, 0, piece)
            all_periods(act, period)

        @block.vector
        def _(dve):
            def combine(triples, count, n, mean_of, part_of, var_of, chain, base, sums, sums_base, scale,
                        summed_ps):
                n_parts = D // count
                mu = triples[:, :, :, 1]
                mean_wide = mean_of.unsqueeze(2).to_broadcast([P, n, n_parts // NR])
                dve.tensor_reduce(part_of, mu, AX_X, ALU.add).then_inc(chain, 1)
                yield
                dve.wait_ge(sums, sums_base + 1)
                dve.tensor_scalar(mean_of, summed_ps, 1.0 / n_parts, None, ALU.mult).then_inc(chain, 1)
                yield
                dve.wait_ge(chain, base + 2)
                dve.tensor_tensor(mu, mu, mean_wide, ALU.subtract).then_inc(chain, 1)
                dve.wait_ge(chain, base + 3)
                dve.tensor_tensor(mu, mu, mu, ALU.mult).then_inc(chain, 1)
                dve.wait_ge(chain, base + 4)
                dve.scalar_tensor_tensor(out=mu, in0=mu, scalar=float(count), in1=triples[:, :, :, 2],
                                         op0=ALU.mult, op1=ALU.add).then_inc(chain, 1)
                dve.wait_ge(chain, base + 5)
                dve.tensor_reduce(part_of, mu, AX_X, ALU.add).then_inc(chain, 1)
                yield
                dve.wait_ge(sums, sums_base + 2)
                dve.tensor_scalar(var_of, summed_ps, scale / D, EPS * scale, ALU.mult, ALU.add).then_inc(chain, 1)
                yield

            def take_stats(dst, tile):
                return dve.bn_stats(dst, tile.rearrange("p g d -> p (g d)"))

            dve.wait_ge(marked, 2 * NR)
            dve.tensor_tensor(fold[:, :], ident[:, 0:DH], ident[:, DH:P], ALU.add).then_inc(folded, 1)
            dve.wait_ge(gated, 1)
            dve.wait_ge(folded, 1)
            dve.tensor_scalar(fold[:, :], fold[:, :], gate[:, 0:1], None, ALU.mult).then_inc(folded, 1)

            dve.wait_ge(x_arrived, 64)
            for j in range(NJ):
                ins = take_stats(stats[:, 0, j, 0, :], x_raw[:, 0, j])
            ins.then_inc(stat_taken, 1)
            dve.wait_ge(stat_taken, 1)
            for _ in combine(stats[:, 0, :, 0, :].rearrange("p j (h s) -> p j h s", s=3), C // 2, NJ,
                             mean[:, 0:NJ], part[:, 0:NJ], var[:, 0:NJ], stat_v, 0, stat_pe, 0, SCALE,
                             m_ps[:, 0:NJ]):
                pass

            def next_norm(b, m, k):
                dve.wait_ge(x_arrived, b * 64 + 64)
                await_(dve, next_rstd, k)
                for i in range(JS):
                    ins = take_stats(next_triples[:, i].rearrange("p h s -> p (h s)"),
                                     x_raw[:, b & 1, bass.ds(m + i * JSTEP, 1)].rearrange("p j g d -> p (j g) d"))
                    if i == JS - 1:
                        ins.then_inc(next_stat, 1)
                    else:
                        yield
                dve.wait_ge(next_stat, k * NSTEPS + 1)
                yield from combine(next_triples[:, :], C // 2, JS, mean[:, bass.ds(b * NJ + m, JS, JSTEP)],
                                   next_part[:, :], next_var[:, :], next_stat, k * NSTEPS + 1, next_sum, k * 2,
                                   SCALE, sums_ps)

            def mask_and_max(n, s):
                dve.wait_ge(scored, n + 1)
                await_(dve, expd, n - 1)
                dve.sem_inc(dve_passed, 1)
                dve.tensor_tensor_reduce(out=neg_scores[s % 2][:, :], in0=s_ps[s % 2][:, 0:T],
                                         in1=mask_sb[:, s % NJ, :], scale=-1.0, scalar=3.0e38, op0=ALU.add,
                                         op1=ALU.min, accum_out=neg_max[:, s:s + 1]).then_inc(masked, 1)

            def lo_parts(g_no, j, norm=None):
                n = g_no * NJ + j
                c = int(j >= CH[0])
                for half in range(2):
                    dve.wait_ge(hi_out[half], n + 1)
                    if norm and half == 1:
                        next(norm)
                    at = (slice(None), j - c * CH[0], slice(half * HALF, (half + 1) * HALF), slice(None))
                    dve.tensor_tensor(pt_lo[c][at], pt_ps[half][0:TT, 0:HALF * P].rearrange("p (t c) -> p t c", c=P),
                                      pt_hi[c][at].bitcast(F32), ALU.subtract).then_inc(lo_out[half], 1)

            def normalize(g_no, slot):
                dve.wait_ge(summed, g_no + 1)
                dve.reciprocal(row_inv[:, :], row_sum[:, slot, :]).then_inc(inverted, 1)
                dve.wait_ge(inverted, g_no + 1)
                await_(dve, added, g_no - 1)
                dve.tensor_tensor(att_n[slot][:, :, :], o_ps[:, 0:NJ * DH].rearrange("p (j d) -> p j d", d=DH),
                                  row_inv[:, :].unsqueeze(2).to_broadcast([P, NJ, DH]), ALU.mult).then_inc(normed, 1)

            def x1_stats(u, tiles):
                if 0 in tiles:
                    dve.wait_ge(added, u * 2 + 2)
                for j in tiles:
                    ins = take_stats(stats[:, (u >> 2) & (B - 1), j, u & 3, :], x1_pair[:, j])
                if NJ - 1 in tiles:
                    ins.then_inc(x1_stat, 1)

            def x1t_out(u):
                dve.wait_ge(xt_filled, u * 2 + 2)
                await_(dve, x1_stored, u * 32)
                dve.tensor_copy(x1t_sb[:, :, :, CH[0]:NJ].rearrange("p r q j -> p j (r q)"),
                                m_ps[:, 0:CH[1] * P].rearrange("p (j c) -> p j c", c=P)).then_inc(xt_dve, 1)

            def period(u, gg, stat):
                g_no = u * 2 + gg
                turn = gg == 1 and exists(u - 1, PAIRS)
                norm = next_norm(*stat) if stat else None
                for j in range(NJ):
                    n = g_no * NJ + j
                    if exists(g_no - 1, GROUPS) and j == 6:
                        normalize(g_no - 1, 1 - gg)
                    if exists(n, TILES):
                        mask_and_max(n, gg * NJ + j)
                    if norm and j in (0, 1, 3, 5):
                        next(norm)
                    if turn and j in (1, 2, 3, 4):
                        x1_stats(u - 1, range(2 * j - 2, min(2 * j, NJ)))
                    if turn and j == 5:
                        x1t_out(u - 1)
                    if exists(n - 2, TILES):
                        lo_parts(g_no - int(j < 2), (j - 2) % NJ, norm if j in (4, 6) else None)

            dve.wait_ge(mask_in, 64)
            all_periods(dve, period)
            dve.wait_ge(x1_stat, PAIRS)
            for _ in combine(stats[:, :, :, :, :].rearrange("p b j n (h s) -> p (b j) (n h) s", s=3), DH, B * NJ,
                             mean[:, :], part[:, :], var[:, :], stat_v, STEPS, stat_pe, 2, 1.0,
                             m_ps[:, 0:B * NJ]):
                pass


def feed_forward(nc, up, down, perm, consts, x1t_dram, stat_dram, zt_dram):
    gate, ones, mean, rstd, var, power = (consts[name] for name in ("gate", "ones", "mean", "rstd", "var", "power"))
    stat_view = stat_dram.rearrange("s (b p j) -> s p b j", b=B, j=NJ)
    BC = B // NC
    UNITS = H * NC
    WCOLS = 2 * M
    with ExitStack() as es:
        def sb(name, shape, dt=F32):
            return es.enter_context(nc.sbuf_tensor(name, shape, dt))

        def sem(name):
            return es.enter_context(nc.semaphore(name))

        perm_sb = sb("perm_sb", [P, H], I32)
        rows_of = [sb(f"rows_of{i}", [P, 1], I32) for i in range(2)]
        mean_w = sb("mean_w", [P, ROWS])
        rstd_w = sb("rstd_w", [P, ROWS])
        xg = [sb(f"xg{i}", [P, ROWS]) for i in range(2)]
        w_raw = [sb(f"w_raw{i}", [P, WCOLS]) for i in range(2)]
        w_hi = [sb(f"w_hi{i}", [P, WCOLS], F32R) for i in range(2)]
        w_lo = [sb(f"w_lo{i}", [P, WCOLS], F32R) for i in range(2)]
        centered = sb("centered", [P, COLS])
        xnorm = [sb(f"xnorm{i}", [P, COLS]) for i in range(2)]
        x_hi = [sb(f"x_hi{i}", [P, COLS], F32R) for i in range(2)]
        x_lo = [sb(f"x_lo{i}", [P, COLS], F32R) for i in range(2)]
        hid = [sb(f"hid{i}", [P, MC, COLS]) for i in range(2)]
        hid_hi = [sb(f"hid_hi{i}", [P, MC, COLS], F32R) for i in range(2)]
        hid_lo = [sb(f"hid_lo{i}", [P, MC, COLS], F32R) for i in range(2)]
        up_ps = [es.enter_context(nc.psum_tensor(f"up_ps{i}", [P, 2, 512], F32)) for i in range(2)]
        dn_ps = es.enter_context(nc.psum_tensor("dn_ps", [P, 512], F32))

        perm_in = sem("perm_in")
        deviated = sem("deviated")
        stat_stored = sem("stat_stored")
        stats_in = sem("stats_in")
        weights_in = [sem(f"weights_in{i}") for i in range(2)]
        rows_set = sem("rows_set")
        gathered = [sem(f"gathered{i}") for i in range(2)]
        scattered = [sem(f"scattered{i}") for i in range(2)]
        weights_cut = sem("weights_cut")
        x_centered = sem("x_centered")
        x_normed = sem("x_normed")
        x_cut = sem("x_cut")
        up_done = sem("up_done")
        gelu_done = sem("gelu_done")
        hid_hi_done = sem("hid_hi_done")
        hid_lo_done = sem("hid_lo_done")
        down_done = sem("down_done")
        z_done = sem("z_done")
        pool_passed = sem("ff_pool_passed")

        block = es.enter_context(nc.Block())

        def cols(c):
            return bass.ds(c * COLS, COLS)

        def run(eng, unit):
            def pair(hp, first=False):
                for hh in range(2):
                    head = hp * 2 + hh
                    unit(head, hh, 0, first and hh == 0)
                    unit(head, hh, 1, first and hh == 0)
                    with eng.Fori(1, NC // 2) as cc:
                        unit(head, hh, cc * 2, False, even=True)
                        unit(head, hh, cc * 2 + 1, False, even=False)
            pair(0, first=True)
            with eng.Fori(1, H // 2) as hp:
                pair(hp)

        @block.sync
        def _(sp):
            sp.dma_start(perm_sb[:, :], perm.rearrange("(h p) -> p h", p=P), allow_slow_non_contiguous=True).then_inc(perm_in, 16)

            def load_weights(head, hh):
                sp.dma_start(w_raw[hh][:, 0:M], up[head]).then_inc(weights_in[hh], 16)
                sp.dma_start(w_raw[hh][:, M:WCOLS].rearrange("p (m d) -> p m d", m=MC),
                             down[head].rearrange("(m p) d -> p m d", p=P)).then_inc(weights_in[hh], 16)

            def tile_rows(t, c):
                return t[0:PJ, c * BC * NJ:(c + 1) * BC * NJ].rearrange("p (b j) -> p b j", j=NJ)

            load_weights(0, 0)
            for c in range(NC):
                sp.wait_ge(deviated, c + 1)
                for k, t in enumerate((mean, rstd)):
                    sp.dma_start(stat_view[k][:, c * BC:(c + 1) * BC], tile_rows(t, c)).then_inc(stat_stored, 16)
                sp.wait_ge(stat_stored, 32 * (c + 1))
                if c > 0:
                    sp.wait_ge(stats_in, 32 * c)
                for k, t in enumerate((mean_w, rstd_w)):
                    sp.dma_start(t[:, cols(c)], stat_dram[k][cols(c)].partition_broadcast(P)).then_inc(stats_in, 16)
                if c == 0:
                    load_weights(1, 1)
            with sp.Fori(1, H // 2) as hp:
                for hh in range(2):
                    sp.wait_ge(weights_cut, hp * 8 - 4 + 4 * hh)
                    load_weights(hp * 2 + hh, hh)

        @block.gpsimd
        def _(pool):
            pool.wait_ge(perm_in, 16)

            def gather(head, hh):
                pool.sem_inc(pool_passed, 1)
                pool.tensor_copy(rows_of[hh][:, :], perm_sb[:, bass.ds(head, 1)]).then_inc(rows_set, 1)
                pool.wait_ge(rows_set, head + 1)
                pool.sem_inc(pool_passed, 1)
                pool.indirect_dma_start(
                    out=xg[hh][:, :], out_offset=None, in_=x1t_dram,
                    in_offset=bass.IndirectOffsetOnAxis(ap=rows_of[hh][:, :].bitcast(U32), axis=0),
                ).then_inc(gathered[hh], 16)

            def scatter(head, hh):
                pool.wait_ge(z_done, (head + 1) * NC)
                pool.sem_inc(pool_passed, 1)
                pool.indirect_dma_start(
                    out=zt_dram, out_offset=bass.IndirectOffsetOnAxis(ap=rows_of[hh][:, :].bitcast(U32), axis=0),
                    in_=xg[hh][:, :], in_offset=None,
                ).then_inc(scattered[hh], 16)

            def cut_weights(head, hh, part, lag):
                at = slice(part * M, (part + 1) * M)
                if part == 0:
                    pool.wait_ge(weights_in[hh], ((head >> 1) + 1) * 32)
                    if lag:
                        pool.wait_ge(down_done, (head - 1) * NC)
                pool.sem_inc(pool_passed, 1)
                pool.tensor_tensor(w_hi[hh][:, at], w_raw[hh][:, at], ones[:, :].to_broadcast([P, M]),
                                   ALU.mult).then_inc(weights_cut, 1)
                pool.wait_ge(weights_cut, head * 4 + part * 2 + 1)
                pool.sem_inc(pool_passed, 1)
                pool.tensor_tensor(w_lo[hh][:, at], w_raw[hh][:, at], w_hi[hh][:, at].bitcast(F32),
                                   ALU.subtract).then_inc(weights_cut, 1)

            def deviation(c):
                at = slice(c * BC * NJ, (c + 1) * BC * NJ)
                pool.tensor_tensor(rstd[:, at], var[:, at], power[:, at], ALU.pow).then_inc(deviated, 1)

            def normalize(head, hh, c, k, par, lag):
                pool.wait_ge(gathered[hh], ((head >> 1) + 1) * 16)
                if lag or c >= 1:
                    pool.wait_ge(x_normed, k)
                pool.sem_inc(pool_passed, 1)
                pool.tensor_tensor(centered[:, :], xg[hh][:, cols(c)], mean_w[:, cols(c)],
                                   ALU.subtract).then_inc(x_centered, 1)
                pool.wait_ge(x_centered, k + 1)
                if lag or c >= 2:
                    pool.wait_ge(x_cut, k * 2 - 2)
                pool.sem_inc(pool_passed, 1)
                pool.tensor_tensor(xnorm[par][:, :], centered[:, :], rstd_w[:, cols(c)],
                                   ALU.mult).then_inc(x_normed, 1)

            gather(0, 0)
            deviation(0)
            cut_weights(0, 0, 0, lag=False)
            cut_weights(0, 0, 1, lag=False)

            def head_units(head, hh, first=False, last=False):
                k = head * NC
                for c in range(3):
                    if first:
                        deviation(c + 1)
                        pool.wait_ge(stats_in, (c + 1) * 32)
                    normalize(head, hh, c, k + c, c % 2, lag=not first)
                if first:
                    gather(1, 1)
                if not last:
                    cut_weights(head + 1, 1 - hh, 0, lag=not first)
                if not first:
                    scatter(head - 1, 1 - hh)
                for c in range(3, 6):
                    if first:
                        deviation(c + 1)
                        pool.wait_ge(stats_in, (c + 1) * 32)
                    normalize(head, hh, c, k + c, c % 2, lag=True)
                if not last:
                    cut_weights(head + 1, 1 - hh, 1, lag=not first)
                if not first and not last:
                    pool.wait_ge(scattered[1 - hh], ((head + 1) >> 1) * 16)
                    gather(head + 1, 1 - hh)
                for c in range(6, NC):
                    if first:
                        if c + 1 < NC:
                            deviation(c + 1)
                        pool.wait_ge(stats_in, (c + 1) * 32)
                    normalize(head, hh, c, k + c, c % 2, lag=True)

            head_units(0, 0, first=True)
            head_units(1, 1)
            with pool.Fori(1, H // 2 - 1) as hp:
                head_units(hp * 2, 0)
                head_units(hp * 2 + 1, 1)
            head_units(H - 2, 0)
            head_units(H - 1, 1, last=True)
            scatter(H - 1, 1)
            pool.wait_ge(scattered[0], 16 * (H // 2))
            pool.wait_ge(scattered[1], 16 * (H // 2))

        @block.tensor
        def _(pe):
            def go_up(hh, k, par, new_head, lag):
                if new_head:
                    pe.wait_ge(weights_cut, (k >> 3) * 4 + 4)
                pe.wait_ge(x_cut, k * 2 + 2)
                for half in range(2):
                    if lag:
                        pe.wait_ge(gelu_done, k * 2 - 1 + half)
                    for i in range(2):
                        m = half * 2 + i
                        dst = up_ps[half][:, i, 0:COLS]
                        pe.matmul(dst, w_hi[hh][:, m * P:(m + 1) * P], x_hi[par][:, :], start=True, stop=False)
                        pe.matmul(dst, w_hi[hh][:, m * P:(m + 1) * P], x_lo[par][:, :], start=False, stop=False)
                        last = pe.matmul(dst, w_lo[hh][:, m * P:(m + 1) * P], x_hi[par][:, :], start=False, stop=True)
                    last.then_inc(up_done, 1)

            def go_down(hh, k, par, lag):
                pe.wait_ge(hid_lo_done, k * 2 + 2)
                if lag:
                    pe.wait_ge(z_done, k)
                for m in range(MC):
                    w = slice(M + m * P, M + (m + 1) * P)
                    pe.matmul(dn_ps[:, 0:COLS], w_hi[hh][:, w], hid_hi[par][:, m, :], start=(m == 0), stop=False)
                    pe.matmul(dn_ps[:, 0:COLS], w_hi[hh][:, w], hid_lo[par][:, m, :], start=False, stop=False)
                    last = pe.matmul(dn_ps[:, 0:COLS], w_lo[hh][:, w], hid_hi[par][:, m, :], start=False,
                                     stop=(m == MC - 1))
                last.then_inc(down_done, 1)

            def unit(head, hh, c, first, even=None):
                k = head * NC + c
                par = c % 2 if even is None else int(not even)
                go_up(hh, k, par, even is None and c == 0, lag=not (first and c == 0))
                if not (first and c == 0):
                    go_down(1 - hh if even is None and c == 0 else hh, k - 1, 1 - par, lag=not (first and c == 1))

            run(pe, unit)
            go_down(1, UNITS - 1, 1, lag=True)

        @block.scalar
        def _(act):
            def unit(head, hh, c, first, even=None):
                k = head * NC + c
                par = c % 2 if even is None else int(not even)
                for half in range(2):
                    at = slice(half * 2, half * 2 + 2)
                    act.wait_ge(up_done, k * 2 + half + 1)
                    if not first:
                        act.wait_ge(hid_lo_done, k * 2 - 3 + half)
                    act.activation(hid[par][:, at, :], up_ps[half][:, :, 0:COLS], ACT.Gelu).then_inc(gelu_done, 1)
                for half in range(2):
                    at = slice(half * 2, half * 2 + 2)
                    act.wait_ge(gelu_done, k * 2 + half + 1)
                    if not first:
                        act.wait_ge(down_done, k - 1)
                    act.activation(hid_hi[par][:, at, :], hid[par][:, at, :], ACT.Copy).then_inc(hid_hi_done, 1)

            run(act, unit)

        @block.vector
        def _(dve):
            def cut_x(k, par, first):
                dve.wait_ge(x_normed, k + 1)
                if not first:
                    dve.wait_ge(up_done, k * 2 - 2)
                dve.tensor_copy(x_hi[par][:, :], xnorm[par][:, :]).then_inc(x_cut, 1)
                dve.wait_ge(x_cut, k * 2 + 1)
                dve.tensor_tensor(x_lo[par][:, :], xnorm[par][:, :], x_hi[par][:, :].bitcast(F32),
                                  ALU.subtract).then_inc(x_cut, 1)

            def cut_hidden(k, par):
                for half in range(2):
                    at = slice(half * 2, half * 2 + 2)
                    dve.wait_ge(hid_hi_done, k * 2 + half + 1)
                    dve.tensor_tensor(hid_lo[par][:, at, :], hid[par][:, at, :], hid_hi[par][:, at, :].bitcast(F32),
                                      ALU.subtract).then_inc(hid_lo_done, 1)

            def result(hh, c, k):
                dve.wait_ge(down_done, k + 1)
                dve.scalar_tensor_tensor(out=xg[hh][:, cols(c)], in0=dn_ps[:, 0:COLS], scalar=gate[:, 1:2],
                                         in1=xg[hh][:, cols(c)], op0=ALU.mult, op1=ALU.add).then_inc(z_done, 1)

            def unit(head, hh, c, first, even=None):
                k = head * NC + c
                par = c % 2 if even is None else int(not even)
                cut_x(k, par, first)
                if not (first and c == 0):
                    cut_hidden(k - 1, 1 - par)
                if not first:
                    back = even is None
                    result(1 - hh if back else hh, c + NC - 2 if back else c - 2, k - 2)

            run(dve, unit)
            cut_hidden(UNITS - 1, 1)
            result(1, NC - 2, UNITS - 2)
            result(1, NC - 1, UNITS - 1)


def transpose_back(nc, consts, zt_dram, out):
    ident = consts["ident"]
    RING = 4
    TILES = ROWS // P
    F = D // P
    zt_view = zt_dram.rearrange("(f p) c -> p f c", p=P)
    out_view = out.rearrange("b q d -> (b q) d")
    with ExitStack() as es:
        z_in = [es.enter_context(nc.sbuf_tensor(f"z_in{i}", [P, F, P], F32)) for i in range(RING)]
        z_out = [es.enter_context(nc.sbuf_tensor(f"z_out{i}", [P, D], F32)) for i in range(RING)]
        z_ps = [es.enter_context(nc.psum_tensor(f"z_ps{i}", [P, D], F32)) for i in range(2)]
        loaded = [es.enter_context(nc.semaphore(f"loaded{i}")) for i in range(RING)]
        stored = [es.enter_context(nc.semaphore(f"stored{i}")) for i in range(RING)]
        turned = es.enter_context(nc.semaphore("z_turned"))
        act_out = es.enter_context(nc.semaphore("z_act_out"))
        dve_out = es.enter_context(nc.semaphore("z_dve_out"))
        block = es.enter_context(nc.Block())

        def ring(eng, tile):
            for s in range(RING):
                tile(s, s, 0, True)
            with eng.Fori(1, TILES // RING) as i:
                for s in range(RING):
                    tile(i * RING + s, s, i, False)

        @block.sync
        def _(sp):
            def tile(i, s, turn, first):
                if not first:
                    sp.wait_ge(turned, i - RING + 1)
                sp.dma_start(z_in[s][:, :, :], zt_view[:, :, bass.ds(i * P, P)]).then_inc(loaded[s], 16)

            ring(sp, tile)

        @block.tensor
        def _(pe):
            def tile(i, s, turn, first):
                pe.wait_ge(loaded[s], turn * 16 + 16)
                if not first or s >= 2:
                    pe.wait_ge(act_out, i - 1)
                    pe.wait_ge(dve_out, i - 1)
                for f in range(F):
                    last = pe.transpose(z_ps[s % 2][:, f * P:(f + 1) * P], z_in[s][:, f, :], ident[:, :])
                last.then_inc(turned, 1)

            ring(pe, tile)

        @block.scalar
        def _(act):
            def tile(i, s, turn, first):
                act.wait_ge(turned, i + 1)
                if not first:
                    act.wait_ge(stored[s], turn * 16)
                act.activation(z_out[s][:, 0:D // 2], z_ps[s % 2][:, 0:D // 2], ACT.Copy).then_inc(act_out, 1)
                act.wait_ge(act_out, i + 1)
                act.wait_ge(dve_out, i + 1)
                act.dma_start(out_view[bass.ds(i * P, P)], z_out[s][:, :]).then_inc(stored[s], 16)

            ring(act, tile)
            for s in range(RING):
                act.wait_ge(stored[s], TILES // RING * 16)

        @block.vector
        def _(dve):
            def tile(i, s, turn, first):
                dve.wait_ge(turned, i + 1)
                if not first:
                    dve.wait_ge(stored[s], turn * 16)
                dve.tensor_copy(z_out[s][:, D // 2:D], z_ps[s % 2][:, D // 2:D]).then_inc(dve_out, 1)

            ring(dve, tile)


_INS = ["x", "ctx_1024", "mask_SxS2_ff0", "g_xattn", "g_ffn", "L0_ffn_up", "L0_ffn_down", "L0_ffn_perm"]
_OUTS = [((B, SQ, D), "float32")]


def kernel(**inputs):
    import numpy as _np
    import concourse.bacc as _bacc
    from concourse import mybir as _mybir
    from concourse.bass_utils import run_bass_kernel_spmd as _run

    nc = _bacc.Bacc("TRN2", target_bir_lowering=False, num_devices=1)
    arrays, args = {}, []
    for name in _INS:
        a = _np.ascontiguousarray(inputs[name])
        arrays[f"in_{name}_dram"] = a
        args.append(nc.dram_tensor(f"in_{name}_dram", a.shape, _mybir.dt.from_np(a.dtype), kind="ExternalInput").ap())
    for i, (shape, dtype) in enumerate(_OUTS):
        dt = _mybir.dt.from_np(_np.dtype(dtype))
        args.append(nc.dram_tensor(f"out_{i}_dram", shape, dt, kind="ExternalOutput").ap())
    build(nc, *args)
    r = _run(nc, [arrays], core_ids=[0])
    return r.results[0]["out_0_dram"]
```
